# Optimizing a Trainium2 kernel written in Bass

```python
import numpy as np
import jax
import jax.numpy as jnp

def _softmax(x, axis=-1):
    return jax.nn.softmax(x, axis=axis)

def _gelu(x):
    return jax.nn.gelu(x, approximate=True)

def _silu(x):
    return jax.nn.silu(x)

def _sigmoid(x):
    return jax.nn.sigmoid(x)

def _layernorm(x, axis=-1, eps=1e-05):
    m = jnp.mean(x, axis=axis, keepdims=True)
    v = jnp.var(x, axis=axis, keepdims=True)
    return (x - m) / jnp.sqrt(v + eps)

def _scatter_add(tgt, idx, src, axis=0):
    return tgt.at[idx].add(src)

def _segment_sum(src, seg, n):
    return jax.ops.segment_sum(src, seg, n)
kernel_name = 'mk_adj_ffn_d1_adj_r2_c0cf47'

def setup_inputs(seed: int=0):
    np.random.seed(seed)
    _w = jnp.asarray

    def _rec_inputs():
        import jax
        import jax.numpy as jnp
        _gk = jax.random.key(seed)
        x = 7.22e-05 + 1 * jax.random.normal(jax.random.fold_in(_gk, 1), (64, 128, 512), jnp.float32)
        _a = jax.random.bernoulli(jax.random.fold_in(_gk, 2), 0.125, (64, 128, 128))
        _a = jnp.logical_or(_a, jnp.swapaxes(_a, -1, -2))
        _a = jnp.logical_or(_a, jnp.eye(128, dtype=bool))
        _af = _a.astype(jnp.float32)
        _af = _af * jax.random.uniform(jax.random.fold_in(_gk, 3), (64, 128, 128), jnp.float32, 0.05, 4.42607)
        adj = _af
        return (x, adj)
    x, adj = _rec_inputs()

    def _L0_gnn_setup():
        import jax, jax.numpy as jnp
        import numpy as np
        NUM_HEADS = 16
        key = jax.random.key(seed)
        ks = jax.random.split(key, 7)
        B, N, D = (16, 256, 512)
        return {'x': jax.random.normal(ks[0], (B, N, D), dtype=jnp.float32), 'spatial_encoding': jax.random.normal(ks[1], (B, N, N), dtype=jnp.float32), 'edge_encoding': jax.random.normal(ks[2], (B, N, N), dtype=jnp.float32), 'Wq': jax.random.normal(ks[3], (D, D), dtype=jnp.float32) * D ** (-0.5), 'Wk': jax.random.normal(ks[4], (D, D), dtype=jnp.float32) * D ** (-0.5), 'Wv': jax.random.normal(ks[5], (D, D), dtype=jnp.float32) * D ** (-0.5), 'Wo': jax.random.normal(ks[6], (D, D), dtype=jnp.float32) * D ** (-0.5)}
    _L0_gnn_all = _L0_gnn_setup()
    _L0_gnn_in = {k: v for k, v in _L0_gnn_all.items() if k in ('Wq', 'Wk', 'Wv', 'Wo')}
    del _L0_gnn_all

    def _L0_ffn_setup():
        import jax, jax.numpy as jnp
        import numpy as np
        B, S, D, E, K = (4, 1024, 512, 8, 2)
        EPS, W_THRES, TEMP = (0.0001, 0.1, 1.0)
        key = jax.random.key(seed)
        k1, k2, k3, k4, k5 = jax.random.split(key, 5)
        x = jax.random.normal(k1, (B, S, D), dtype=jnp.float32)
        gate_W = jax.random.normal(k2, (D, E), dtype=jnp.float32) * 0.02
        gate_b = jnp.zeros((E,), dtype=jnp.float32)
        expert_W = jax.random.normal(k3, (E, D, D), dtype=jnp.float32) * 0.02
        expert_b = jnp.zeros((E, D), dtype=jnp.float32)
        return {'x': x, 'gate_W': gate_W, 'gate_b': gate_b, 'expert_W': expert_W, 'expert_b': expert_b}
    _L0_ffn_all = _L0_ffn_setup()
    _L0_ffn_in = {k: v for k, v in _L0_ffn_all.items() if k in ('gate_W', 'gate_b', 'expert_W', 'expert_b')}
    del _L0_ffn_all
    return {'x': x, 'adj': adj, 'L0_gnn_Wq': _L0_gnn_in['Wq'], 'L0_gnn_Wk': _L0_gnn_in['Wk'], 'L0_gnn_Wv': _L0_gnn_in['Wv'], 'L0_gnn_Wo': _L0_gnn_in['Wo'], 'L0_ffn_gate_W': _L0_ffn_in['gate_W'], 'L0_ffn_gate_b': _L0_ffn_in['gate_b'], 'L0_ffn_expert_W': _L0_ffn_in['expert_W'], 'L0_ffn_expert_b': _L0_ffn_in['expert_b']}

def reference(x, adj, L0_gnn_Wq, L0_gnn_Wk, L0_gnn_Wv, L0_gnn_Wo, L0_ffn_gate_W, L0_ffn_gate_b, L0_ffn_expert_W, L0_ffn_expert_b):
    import jax
    import jax.numpy as jnp

    def _L0_gnn_ref(x, spatial_encoding, edge_encoding, Wq, Wk, Wv, Wo):
        import jax, jax.numpy as jnp
        import numpy as np
        NUM_HEADS = 16
        B, N, D = x.shape
        H = NUM_HEADS
        hd = D // H
        scale = D ** (-0.5)

        def split_heads(t):
            return t.reshape(B, N, H, hd).transpose(0, 2, 1, 3)
        q = split_heads(x @ Wq.T)
        k = split_heads(x @ Wk.T)
        v = split_heads(x @ Wv.T)
        bias = (spatial_encoding + edge_encoding)[:, None]
        a = jnp.einsum('bhnd,bhmd->bhnm', q, k) * scale + bias
        row_nonzero = jnp.any(a != 0, axis=-1, keepdims=True)
        a = jnp.where(row_nonzero, a, -jnp.inf)
        p = jax.nn.softmax(a, axis=-1)
        p = jnp.where(jnp.isnan(p), 0.0, p)
        o = jnp.einsum('bhnm,bhmd->bhnd', p, v)
        o = o.transpose(0, 2, 1, 3).reshape(B, N, D)
        return o @ Wo.T

    def _L0_ffn_ref(x, gate_W, gate_b, expert_W, expert_b):
        import jax, jax.numpy as jnp
        import numpy as np
        B, S, D, E, K = (4, 1024, 512, 8, 2)
        EPS, W_THRES, TEMP = (0.0001, 0.1, 1.0)
        scores = jnp.maximum((x @ gate_W + gate_b) / TEMP, EPS)
        p = jax.nn.softmax(scores, axis=-1)
        _, topk_idx = jax.lax.top_k(p, K)
        topk_mask = jax.nn.one_hot(topk_idx, E, dtype=p.dtype).sum(-2) > 0
        w = jnp.maximum(p, W_THRES)
        w_gather = jnp.take_along_axis(w, topk_idx, axis=-1)
        total = jax.lax.stop_gradient(w_gather.sum(-1, keepdims=True))
        w = w / total
        comb = jnp.where(topk_mask, w, jnp.zeros_like(w))
        y = jnp.einsum('bsd,edf->bsef', x, expert_W) + expert_b
        out = jnp.einsum('bsef,bse->bsf', y, comb) / K
        return out
    x = x + _L0_gnn_ref(_layernorm(x, axis=-1), adj, adj, L0_gnn_Wq, L0_gnn_Wk, L0_gnn_Wv, L0_gnn_Wo)
    x = x + _L0_ffn_ref(_layernorm(x, axis=-1), L0_ffn_gate_W, L0_ffn_gate_b, L0_ffn_expert_W, L0_ffn_expert_b)
    return x

_drawn_inputs = setup_inputs


def setup_inputs(seed=0):
    import zlib

    import numpy as np

    out = dict(_drawn_inputs(seed))
    spreads = {'L0_ffn_gate_b': (0.0, 0.1), 'L0_ffn_expert_b': (0.0, 0.1)}
    factors = {}
    for name, (base, spread) in spreads.items():
        noise = np.random.default_rng([zlib.crc32(name.encode()), seed]).standard_normal(out[name].shape)
        drawn = base * np.exp(spread * noise) if base else spread * noise
        out[name] = jnp.asarray(drawn.astype(out[name].dtype))
    for name, factor in factors.items():
        out[name] = (out[name] * factor).astype(out[name].dtype)
    return out
```

```python
import numpy as np
import concourse.bass as bass
from concourse import mybir
from contextlib import ExitStack

P = 128
B = 64
D = 512
DC = D // P
H = 16
HD = D // H
HC = P // HD
E = 8
K = 2
SCALE = float(D) ** -0.5
LN_EPS = 1e-5
GATE_EPS = 1e-4
W_THRES = 0.1
BIG = 3e38

T = B * P
LIST = T + P
TILES = T * K // P + E - 1
SPARE = (E - 1) * P
ROWS = E * LIST + SPARE
W = D + 1 + E
RING = 3
DUMMY = (1 + E - 1) * P

C_ID, C_SEL, C_REV, C_BASE, C_ROW, C_TRI = 0, P, P + E, P + E + 2 * E, P + 2 * E + 2 * E, P + 4 * E + 1
C_MULT = C_TRI + P
C_TILE = C_MULT + B
C_DEP = C_TILE + TILES
C_TOK = C_DEP + TILES
C_DUM = C_TOK + B
C_ALL = C_DUM + E


class Item:

    def __init__(self, g, per, off, n):
        self.g, self.per, self.off, self.n = g, per, off, n

    @property
    def valid(self):
        return not isinstance(self.g, int) or 0 <= self.per * self.g + self.off < self.n

    def after(self, before):
        return not isinstance(self.g, int) or self.per * self.g + self.off >= before

    def count(self, m=1, t=0):
        return m * self.per * self.g + (m * self.off + t)

    def ring(self, n):
        return self.off % n

    def turn(self, n):
        return (self.per // n) * self.g + self.off // n


def build(nc, x, adj, WqT, WkT, WvT, WoT, gate_W, gate_b, expert_W, expert_b, consts, out):
    f32, f32r, bf16, i32 = mybir.dt.float32, mybir.dt.float32r, mybir.dt.bfloat16, mybir.dt.int32
    ALU, ACT, AX = mybir.AluOpType, mybir.ActivationFunctionType, mybir.AxisListType

    x_lists = nc.dram_tensor("x_lists", [ROWS, W], f32, kind="Internal").ap()
    e_parts = nc.dram_tensor("e_parts", [2, E * DC, P, D], f32, kind="Internal").ap()

    top = ExitStack()
    with top:
        def sb(stack, name, shape, dt=f32):
            return stack.enter_context(nc.sbuf_tensor(name, shape, dt))

        def pb(stack, name, shape, dt=f32):
            return stack.enter_context(nc.psum_tensor(name, shape, dt))

        def sem(name):
            return top.enter_context(nc.semaphore(name))

        def sems(name, n):
            return [sem(f"{name}{i}") for i in range(n)]

        const = sb(top, "const", [P, C_ALL])
        ident = const[:, C_ID:C_ID + P]
        fill = sb(top, "fill", [P, 2, E])
        ends = sb(top, "ends", [1, E], i32)
        zero_tile = sb(top, "zero_tile", [P, W])
        const_in = sem("const_in")
        fill_done = sem("fill_done")

        phase_a(nc, locals())
        phase_b(nc, locals())


def phase_a(nc, v):
    f32, f32r, bf16, i32 = v["f32"], v["f32r"], v["bf16"], v["i32"]
    ALU, ACT, AX = v["ALU"], v["ACT"], v["AX"]
    sem, sems = v["sem"], v["sems"]
    const, ident, fill, ends, zero_tile = v["const"], v["ident"], v["fill"], v["ends"], v["zero_tile"]
    const_in, fill_done = v["const_in"], v["fill_done"]
    x, adj, x_lists, e_parts, out = v["x"], v["adj"], v["x_lists"], v["e_parts"], v["out"]

    mem = ExitStack()
    with mem:
        def sb(name, shape, dt=f32):
            return v["sb"](mem, name, shape, dt)

        def pb(name):
            return v["pb"](mem, name, [P, 512], f32)

        w_hi = {n: sb(f"w{n}_hi", [P, DC, D], f32r) for n in "kqvo"}
        w_lo = {n: sb(f"w{n}_lo", [P, DC, D], f32r) for n in "kqvo"}
        gate_w = sb("gate_w", [P, DC, HD])
        gate_bias = sb("gate_bias", [P, E])
        tri = sb("tri", [P, P], bf16)
        ones = sb("ones", [P, P], bf16)
        half = sb("half", [P, 2])
        xin = sb("xin", [P, 4, D])
        xres = sb("xres", [P, 2, D])
        bias = sb("bias", [P, 4, P])
        xT_hi = sb("xT_hi", [P, 2, DC, 2 * P], f32r)
        xT_lo = sb("xT_lo", [P, 2, DC, 2 * P], f32r)
        qT = sb("qT", [P, 2, DC, 2 * P])
        kT = sb("kT", [P, 2, DC, 2 * P])
        kblk = sb("kblk", [P, 2, DC, HC * P])
        vv = sb("vv", [P, 4, D])
        prob = sb("prob", [P, 2, DC, HC, P])
        pT = sb("pT", [P, 2, HC, P])
        nmax, amax, rsum, rinv = (sb(n, [P, 2, H]) for n in ("nmax", "amax", "rsum", "rinv"))
        oT_hi = sb("oT_hi", [P, 2, DC, P], f32r)
        oT_lo = sb("oT_lo", [P, 2, DC, P], f32r)
        xn2 = sb("xn2", [P, 4, W])
        xn2T = sb("xn2T", [P, DC, 2 * P])
        st1, st2 = sb("st1", [P, 4, 6]), sb("st2", [P, 4, 6])
        mv1, mv2 = sb("mv1", [P, 4, 2]), sb("mv2", [P, 4, 2])
        var1, nwt1, rstd1 = (sb(n, [P, 4]) for n in ("var1", "nwt1", "rstd1"))
        var2, nwt2, rstd2 = (sb(n, [P, 4]) for n in ("var2", "nwt2", "rstd2"))
        gT = sb("gT", [P, 2 * P])
        score, dlt, eexp, eq, key, score2, em = (sb(n, [P, 2, E]) for n in ("score", "dlt", "eexp", "eq", "key", "score2", "em"))
        mask = sb("mask", [P, K, 2, E])
        mask_sum = sb("mask_sum", [P, 3, E], bf16)
        m1, m2, kmax, den, e2 = (sb(n, [P, 2]) for n in ("m1", "m2", "kmax", "den", "e2"))
        wgt = sb("wgt", [P, K, 2])
        wtot = sb("wtot", [P, 2])
        place = sb("place", [P, 2, E])
        place_k = sb("place_k", [P, K, 2, E])
        posf = sb("posf", [P, K, 2])
        pos = sb("pos", [P, 2, K, 2], i32)
        comb_k = sb("comb_k", [P, K, 2, E])
        spare_end = sb("spare_end", [P, E - 1, 1 + E])
        e_stage = sb("e_stage", [P, D])
        e_hi = sb("e_hi", [P, D], f32r)
        e_lo = sb("e_lo", [P, D], f32r)

        ps_s = [pb("ps_s0"), pb("ps_s1")]
        ps_t = [pb("ps_t0"), pb("ps_t1")]
        ps_o = pb("ps_o")
        ps_p = [pb("ps_p0"), pb("ps_p1")]
        ps_g = pb("ps_g")
        G_T, G_S, G_P = ps_g[:, 0:2 * P], ps_g[:, 2 * P:2 * P + 2 * E], ps_g[:, 3 * P:3 * P + 3 * E]

        stage_in = sems("stage_in", 2)
        small_in = sem("small_in")
        w_hi_done, w_lo_done = sem("w_hi_done"), sem("w_lo_done")
        zeroed, consts_done = sem("zeroed"), sem("consts_done")
        x_in, bias_in = sems("x_in", 4), sems("bias_in", 4)
        xres_in, x1_out = sems("xres_in", 2), sems("x1_out", 2)
        kblk_in = sems("kblk_in", 2)
        spare_out = sem("spare_out")
        e_in, e_hi_done, e_lo_done, e_out = sem("e_in"), sem("e_hi_done"), sem("e_lo_done"), sem("e_out")
        bias_done = sem("bias_done")
        stats1, mean1, rstd1_step, xn_done = sem("stats1"), sem("mean1"), sem("rstd1_step"), sem("xn_done")
        stats2, mean2, rstd2_step, xn2_done = sem("stats2"), sem("mean2"), sem("rstd2_step"), sem("xn2_done")
        proj_full = {k: sem(f"{k}_full") for k in ("K", "Q", "V", "X", "O", "X2")}
        xT_hi_done, xT_lo_done = sem("xT_hi_done"), sem("xT_lo_done")
        k_done, q_done, v_done = sem("k_done"), sem("q_done"), sem("v_done")
        s_full, s_read, absmax_done, exp_done = sem("s_full"), sem("s_read"), sem("absmax_done"), sem("exp_done")
        rinv_step, prob_done = sem("rinv_step"), sem("prob_done")
        pT_full, pT_done, pv_done = sem("pT_full"), sem("pT_done"), sem("pv_done")
        oT_hi_done, oT_lo_done = sem("oT_hi_done"), sem("oT_lo_done")
        x1_done, xn2T_done = sem("x1_done"), sem("xn2T_done")
        gate_full, gT_done, gsum_full, gexp_done = sem("gate_full"), sem("gT_done"), sem("gsum_full"), sem("gexp_done")
        route_step, place_full, place_step = sem("route_step"), sem("place_full"), sem("place_step")
        scattered = sems("scattered", 2)
        half_done = sem("half_done")
        pool_held = sem("pool_held")
        dve_held, sp_held = sem("dve_held"), sem("sp_held")

        def graph(g, off):
            return Item(g, 4, off, B)

        def pair(g, off):
            return Item(g, 2, off // 2, B // 2)

        QUARTERS = ([[("K", 2, 0)], [("K", 2, 1), ("X2", -3, 0)], [("O", -2, 0)], [("Q", 2, 0)]],
                    [[("Q", 1, 1)], [("V", 1, 0), ("X", 3, 0)], [("O", -2, 0), ("X", 3, 1)], [("V", 1, 1), ("X2", -3, 0)]])
        EVEN, ODD = (sum(q, []) for q in QUARTERS)

        def uses(j, c):
            before = sum(len(q) for q in QUARTERS[j % 2][:c])
            return list(range(before, before + len(QUARTERS[j % 2][c])))

        def number(j, kind, part=0):
            return [(k, p) for k, _, p in (ODD if j % 2 else EVEN)].index((kind, part))

        PER = len(EVEN) + len(ODD)
        READ_BY = {"K": k_done, "Q": q_done, "V": v_done, "X": xT_lo_done, "O": x1_done, "X2": xn2T_done}

        def use(g, j, n):
            kind, lag, part = (ODD if j % 2 else EVEN)[n]
            if kind in ("O", "X2"):
                it = graph(g, j + lag)
                return kind, it, part, it.count(1, 1)
            it = pair(g, j + lag)
            return kind, it, part, it.count(2, part + 1)

        def bank_of(j, n):
            return (n + (len(EVEN) if j % 2 else 0)) % 2

        def bank_free(g, j, n):
            jj, nn = j, n
            for _ in range(4 * PER):
                nn -= 1
                if nn < 0:
                    jj -= 1
                    nn = len(ODD if jj % 2 else EVEN) - 1
                if bank_of(jj, nn) != bank_of(j, n):
                    continue
                kind, it, part, count = use(g, jj, nn)
                if it.valid:
                    return READ_BY[kind], count
            return None

        FIRST, LAST = -2, 17
        LOOP = (3, 14)

        def turns(eng, body, after_first=None):
            for g in range(FIRST, LOOP[0]):
                body(g)
                if g == FIRST and after_first:
                    after_first()
            with eng.Fori(LOOP[0], LOOP[1]) as g:
                body(g)
            for g in range(LOOP[1], LAST + 1):
                body(g)

        RSTD, ROUTE, PLACE = 6, 24, 4

        block = mem.enter_context(nc.Block())

        @block.sync
        def _(sp):
            sp.dma_start(const[:, :], v["consts"]).then_inc(const_in, 16)
            sp.wait_ge(zeroed, 1)
            sp.dma_start(gate_w[:, :, 0:E], v["gate_W"].rearrange("(c p) e -> p c e", p=P)).then_inc(small_in, 16)
            sp.dma_start(gate_bias[:, :], v["gate_b"].rearrange("(a e) -> a e", a=1).to_broadcast([P, E])).then_inc(small_in, 16)
            sp.wait_ge(zeroed, 3)

            def hold(semaphore, value):
                sp.wait_ge(semaphore, value)
                sp.sem_inc(sp_held, 1)

            def body(g):
                for j in range(4):
                    b = graph(g, j + 1)
                    if b.valid:
                        hold(k_done, pair(g, j + 1).count(2, 2))
                        if b.after(2):
                            hold(s_full, b.count(4, -4))
                        r, q = b.ring(2), pair(g, j + 1).ring(2)
                        for h in range(HC):
                            rows = slice(HD * h, HD * h + HD)
                            sp.dma_start(kblk[rows, r, :, P * h:P * h + P], kT[rows, q, :, P * r:P * r + P]).then_inc(kblk_in[r], 16)
                    b = graph(g, j + 6)
                    if b.valid:
                        if b.after(4):
                            hold(proj_full["X"], pair(g, j + 6).count(2, -2))
                        sp.dma_start(xin[:, b.ring(4), :], x[bass.ds(b.count(), 1)].rearrange("a p d -> (a p) d")).then_inc(x_in[b.ring(4)], 16)
                    b = graph(g, j + 2)
                    if b.valid:
                        if b.after(4):
                            hold(s_read, b.count(4, -12))
                        sp.dma_start(bias[:, b.ring(4), :], adj[bass.ds(b.count(), 1)].rearrange("a p d -> (a p) d")).then_inc(bias_in[b.ring(4)], 16)
                    b = graph(g, j - 3)
                    if b.valid:
                        hold(x1_done, b.count(1, 1))
                        sp.dma_start(out[bass.ds(b.count(P), P), :], xres[:, b.ring(2), :]).then_inc(x1_out[b.ring(2)], 16)
                    p = pair(g, j - 6)
                    if p.valid and j % 2 == 0:
                        hold(e_lo_done, p.count(1, 1))
                        for i, part in enumerate((e_hi, e_lo)):
                            sp.dma_start(e_parts[i, bass.ds(p.count(), 1)].rearrange("a p d -> (a p) d"), part[:, :].bitcast(f32)).then_inc(e_out, 16)
                    p = pair(g, j - 4)
                    if p.valid and j % 2 == 0:
                        sp.dma_start(e_stage[:, :], v["expert_W"].rearrange("e d f -> (e d) f")[bass.ds(p.count(P), P), :]).then_inc(e_in, 16)
                    b = graph(g, j - 1)
                    if b.valid:
                        if b.after(2):
                            hold(xn2_done, b.count(1, -1))
                            hold(x1_out[b.ring(2)], 16 * b.turn(2))
                        sp.dma_start(xres[:, b.ring(2), :], x[bass.ds(b.count(), 1)].rearrange("a p d -> (a p) d")).then_inc(xres_in[b.ring(2)], 16)

            turns(sp, body)
            sp.wait_ge(spare_out, 48)
            sp.wait_ge(e_out, 32 * E * DC)
            for r in range(2):
                sp.wait_ge(x1_out[r], 16 * (B // 2))

        @block.tensor
        def _(pe):
            mm = nc.tensor.matmul

            def three(out_, lhs_hi, lhs_lo, rhs_hi, rhs_lo, first, last):
                mm(out_, lhs_hi, rhs_hi, start=first, stop=False)
                mm(out_, lhs_hi, rhs_lo, start=False, stop=False)
                return mm(out_, lhs_lo, rhs_hi, start=False, stop=last)

            def wait_bank(g, j, n):
                free = bank_free(g, j, n)
                if free:
                    pe.wait_ge(*free)

            def work(g, j, n):
                kind, it, part, count = use(g, j, n)
                if not it.valid:
                    return
                bank = ps_p[bank_of(j, n)]
                if kind in ("K", "Q"):
                    pe.wait_ge(xT_lo_done, it.count(2, 2))
                    if isinstance(g, int) and 2 * g + it.off == 0:
                        pe.wait_ge(w_lo_done, 1 if kind == "K" else 2)
                    wait_bank(g, j, n)
                    r, w = it.ring(2), kind.lower()
                    for oc in range(2):
                        o = P * (2 * part + oc)
                        for c in range(DC):
                            last = three(bank[:, 2 * P * oc:2 * P * oc + 2 * P], w_hi[w][:, c, o:o + P], w_lo[w][:, c, o:o + P],
                                         xT_hi[:, r, c, :], xT_lo[:, r, c, :], c == 0, c == DC - 1)
                elif kind == "V":
                    if isinstance(g, int) and 2 * g + it.off == 0:
                        pe.wait_ge(w_lo_done, 3)
                    wait_bank(g, j, n)
                    r, t = it.ring(2), slice(P * part, P * part + P)
                    for c in range(DC):
                        last = three(bank[:, :], xT_hi[:, r, c, t], xT_lo[:, r, c, t], w_hi["v"][:, c, :], w_lo["v"][:, c, :], c == 0, c == DC - 1)
                elif kind == "O":
                    pe.wait_ge(oT_lo_done, it.count(1, 1))
                    if isinstance(g, int) and 4 * g + it.off == 0:
                        pe.wait_ge(w_lo_done, 4)
                    wait_bank(g, j, n)
                    r = it.ring(2)
                    for c in range(DC):
                        last = three(bank[:, :], oT_hi[:, r, c, :], oT_lo[:, r, c, :], w_hi["o"][:, c, :], w_lo["o"][:, c, :], c == 0, c == DC - 1)
                elif kind == "X":
                    pe.wait_ge(xn_done, it.count(2, 2))
                    wait_bank(g, j, n)
                    for cc in range(2):
                        c = 2 * part + cc
                        for r in range(2):
                            last = nc.tensor.transpose(bank[:, P * (2 * cc + r):P * (2 * cc + r) + P],
                                                       xin[:, 2 * it.ring(2) + r, P * c:P * c + P], ident)
                else:
                    pe.wait_ge(xn2_done, it.count(1, 1))
                    wait_bank(g, j, n)
                    for c in range(DC):
                        last = nc.tensor.transpose(bank[:, P * c:P * c + P], xn2[:, it.ring(4), P * c:P * c + P], ident)
                last.then_inc(proj_full[kind], 1)

            def scores(b, p, c):
                if c == 0:
                    pe.wait_ge(kblk_in[b.ring(2)], 64 * b.turn(2) + 64)
                    pe.wait_ge(q_done, p.count(2, 2))
                if b.after(1) or c >= 2:
                    pe.wait_ge(s_read, b.count(4, c - 1))
                mm(ps_s[c % 2][:, :], qT[:, p.ring(2), c, P * b.ring(2):P * b.ring(2) + P], kblk[:, b.ring(2), c, :],
                   start=True, stop=True).then_inc(s_full, 1)

            def transpose_probs(b, c):
                pe.wait_ge(prob_done, b.count(4, c + 1))
                if b.after(1) or c >= 2:
                    pe.wait_ge(pT_done, b.count(4, c - 1))
                for h in range(HC):
                    last = nc.tensor.transpose(ps_t[c % 2][:, P * h:P * h + P], prob[:, b.ring(2), c, h, :], ident)
                last.then_inc(pT_full, 1)

            def times_v(b, c):
                pe.wait_ge(pT_done, b.count(4, c + 1))
                if c == 0:
                    pe.wait_ge(v_done, b.count(1, 1))
                    if b.after(1):
                        pe.wait_ge(oT_lo_done, b.count(1, 0))
                for h in range(HC):
                    last = mm(ps_o[HD * h:HD * h + HD, P * c:P * c + P], vv[:, b.ring(4), HD * (HC * c + h):HD * (HC * c + h) + HD],
                              pT[:, c % 2, h, :], start=True, stop=True)
                last.then_inc(pv_done, 1)

            def attend(g, j, c):
                b = graph(g, j - 1 if c else j - 2)
                if b.valid:
                    times_v(b, (c - 1) % DC)

            pe.wait_ge(const_in, 16)

            def body(g):
                for j in range(4):
                    for c in range(DC):
                        b = graph(g, j)
                        if b.valid:
                            scores(b, pair(g, j), c)
                        for i, n in enumerate(uses(j, c)):
                            if i == 1:
                                attend(g, j, c)
                            work(g, j, n)
                        if len(uses(j, c)) == 1:
                            attend(g, j, c)
                        if c == 3 and j % 2 == 0:
                            p = pair(g, j - 4)
                            if p.valid:
                                pe.wait_ge(xn2T_done, p.count(2, 2))
                                if isinstance(g, int) and 2 * g + p.off == 0:
                                    pe.wait_ge(small_in, 32)
                                if p.after(1):
                                    pe.wait_ge(place_step, p.count(PLACE, -PLACE + 1))
                                for cc in range(DC):
                                    last = mm(ps_g[HD * cc:HD * cc + HD, 0:2 * P], gate_w[:, cc, :], xn2T[:, cc, :], start=True, stop=True)
                                last.then_inc(gate_full, 1)
                        if c == 1 and j % 2:
                            p = pair(g, j - 5)
                            if p.valid:
                                pe.wait_ge(gT_done, p.count(1, 1))
                                for r in range(2):
                                    last = mm(G_S[:, E * r:E * r + E], gT[:, P * r:P * r + P], const[:, C_SEL:C_SEL + E], start=True, stop=True)
                                last.then_inc(gsum_full, 1)
                        if c == 0 and j % 2 == 0:
                            p = pair(g, j - 6)
                            if p.valid:
                                pe.wait_ge(route_step, p.count(ROUTE, 15))
                                if isinstance(g, int) and 2 * g + p.off == 0:
                                    pe.wait_ge(consts_done, 3)
                                mm(G_P, tri[:, :], mask_sum[:, :, :].rearrange("p a e -> p (a e)"), start=True, stop=False)
                                mm(G_P[:, E:3 * E], ones[:, :], mask_sum[:, 0:2, :].rearrange("p a e -> p (a e)"), start=False, stop=False)
                                mm(G_P[:, 2 * E:3 * E], ones[:, :], mask_sum[:, 0, :], start=False, stop=True).then_inc(place_full, 1)
                        b = graph(g, j - 1)
                        if b.valid:
                            transpose_probs(b, c)

            turns(pe, body)

        @block.scalar
        def _(act):
            wide = {n: w.rearrange("(c p) o -> p c o", p=P) for n, w in
                    (("k", v["WkT"]), ("q", v["WqT"]), ("v", v["WvT"]), ("o", v["WoT"]))}

            def matrix_in(i, n):
                act.dma_start(prob[:, i % 2].rearrange("p c h m -> p c (h m)"), wide[n]).then_inc(stage_in[i % 2], 16)

            def matrix_hi(i, n):
                act.wait_ge(stage_in[i % 2], 16 * (i // 2) + 16)
                nc.scalar.activation(w_hi[n][:, :, :], prob[:, i % 2].rearrange("p c h m -> p c (h m)"), ACT.Copy).then_inc(w_hi_done, 1)

            matrix_in(0, "k")
            matrix_in(1, "q")
            matrix_hi(0, "k")
            matrix_hi(1, "q")
            for i, n in ((2, "v"), (3, "o")):
                act.wait_ge(w_lo_done, i - 1)
                matrix_in(i, n)

            def after_first():
                matrix_hi(2, "v")
                matrix_hi(3, "o")
                act.wait_ge(zeroed, 2)
                act.wait_ge(consts_done, 6)
                spare = x_lists[E * LIST:ROWS, :].rearrange("(n p) d -> p n d", p=P)
                act.dma_start(spare[:, :, 0:D], zero_tile[:, 0:D].unsqueeze(1).to_broadcast([P, E - 1, D])).then_inc(spare_out, 16)
                act.dma_start(spare[:, :, D:W], spare_end[:, :, :]).then_inc(spare_out, 16)
                act.dma_start(out[T:T + DUMMY, :].rearrange("(n p) d -> p n d", p=P), zero_tile[:, 0:D].unsqueeze(1).to_broadcast([P, E, D])).then_inc(spare_out, 16)

            def read(g, j, n):
                kind, it, part, count = use(g, j, n)
                if not it.valid or kind == "O":
                    return
                bank = ps_p[bank_of(j, n)]
                act.wait_ge(proj_full[kind], count)
                r = it.ring(2)
                if kind == "K":
                    if it.after(2):
                        for k in range(2):
                            act.wait_ge(kblk_in[k], it.count(64, -64))
                    nc.scalar.activation(kT[:, r, 2 * part:2 * part + 2, :].rearrange("p c t -> p (c t)"), bank[:, :], ACT.Copy).then_inc(k_done, 1)
                elif kind == "Q":
                    if it.after(2):
                        act.wait_ge(s_full, it.count(8, -8))
                    nc.scalar.activation(qT[:, r, 2 * part:2 * part + 2, :].rearrange("p c t -> p (c t)"), bank[:, :], ACT.Copy, scale=SCALE).then_inc(q_done, 1)
                elif kind == "V":
                    if it.after(2):
                        act.wait_ge(pv_done, it.count(8, 4 * part - 12))
                    nc.scalar.activation(vv[:, 2 * r + part, :], bank[:, :], ACT.Copy).then_inc(v_done, 1)
                elif kind == "X":
                    if it.after(2):
                        act.wait_ge(proj_full["V"], it.count(2, -2))
                    nc.scalar.activation(xT_hi[:, r, 2 * part:2 * part + 2, :].rearrange("p c t -> p (c t)"), bank[:, :], ACT.Copy).then_inc(xT_hi_done, 1)
                else:
                    p = pair(g, j - 3)
                    if p.after(1):
                        act.wait_ge(gate_full, p.count())
                    r = it.ring(2)
                    nc.scalar.activation(xn2T[:, :, P * r:P * r + P], bank[:, :].rearrange("p (c t) -> p c t", c=DC), ACT.Copy).then_inc(xn2T_done, 1)

            def body(g):
                for j in range(4):
                    p = pair(g, j - 4)
                    if p.valid and j % 2:
                        act.wait_ge(e_in, p.count(16, 16))
                        if p.after(1):
                            act.wait_ge(e_out, p.count(32))
                        nc.scalar.activation(e_hi[:, :], e_stage[:, :], ACT.Copy).then_inc(e_hi_done, 1)
                    for c in range(DC):
                        b = graph(g, j)
                        if b.valid:
                            act.wait_ge(absmax_done, b.count(4, c + 1))
                            r = b.ring(2)
                            if b.after(2) and c == 0:
                                act.wait_ge(rinv_step, b.count(2, -2))
                            for h in range(HC):
                                n = HC * c + h
                                last = nc.scalar.activation(prob[:, r, c, h, :], prob[:, r, c, h, :], ACT.Exp, bias=nmax[:, r, n:n + 1],
                                                            scale=-1.0, accum_out=rsum[:, r, n:n + 1])
                            last.then_inc(exp_done, 1)
                        n = uses(j, c)
                        read(g, j, n[0])
                        if c == 0:
                            b = graph(g, j - 2)
                            if b.valid:
                                act.wait_ge(pv_done, b.count(4, 4))
                                if b.after(2):
                                    act.wait_ge(proj_full["O"], b.count(1, -1))
                                nc.scalar.activation(oT_hi[:, b.ring(2)].rearrange("p c t -> p (c t)"), ps_o[:, :], ACT.Copy).then_inc(oT_hi_done, 1)
                            if j % 2:
                                p = pair(g, j - 5)
                                if p.valid:
                                    act.wait_ge(gate_full, p.count(1, 1))
                                    if p.after(1):
                                        act.wait_ge(gsum_full, p.count())
                                    nc.scalar.activation(gT[:, :], G_T, ACT.Copy).then_inc(gT_done, 1)
                        if len(n) == 2:
                            read(g, j, n[1])
                        if c == 3 and j % 2:
                            p = pair(g, j - 5)
                            if p.valid:
                                act.wait_ge(route_step, p.count(ROUTE, 4))
                                if p.after(1):
                                    act.wait_ge(route_step, p.count(ROUTE))
                                nc.scalar.activation(eexp[:, :, :], dlt[:, :, :], ACT.Exp).then_inc(gexp_done, 1)
                        b = graph(g, j - 1)
                        if b.valid:
                            act.wait_ge(pT_full, b.count(4, c + 1))
                            if b.after(1) or c >= 2:
                                act.wait_ge(pv_done, b.count(4, c - 1))
                            nc.scalar.activation(pT[:, c % 2].rearrange("p h t -> p (h t)"), ps_t[c % 2][:, :], ACT.Copy).then_inc(pT_done, 1)

            turns(act, body, after_first)

        @block.vector
        def _(dve):
            tt, ts = nc.vector.tensor_tensor, nc.vector.tensor_scalar
            nc.vector.memset(gate_w[:, :, :], 0.0).then_inc(zeroed, 1)
            nc.vector.memset(zero_tile[:, :], 0.0).then_inc(zeroed, 1)
            nc.vector.memset(kblk[:, :, :, :], 0.0).then_inc(zeroed, 1)
            nc.vector.memset(mask_sum[:, :, :], 0.0).then_inc(consts_done, 1)
            nc.vector.memset(ones[:, :], 1.0).then_inc(consts_done, 1)
            dve.wait_ge(const_in, 16)
            nc.vector.tensor_copy(tri[:, :], const[:, C_TRI:C_TRI + P]).then_inc(consts_done, 1)
            nc.vector.tensor_copy(fill[:, 0, :], const[:, C_BASE:C_BASE + E]).then_inc(consts_done, 1)
            nc.vector.memset(spare_end[:, :, 1:1 + E], 0.0).then_inc(consts_done, 1)
            nc.vector.tensor_copy(spare_end[:, :, 0], const[:, C_DUM + 1:C_DUM + E]).then_inc(consts_done, 1)
            dve.wait_ge(zeroed, 2)
            nc.vector.tensor_copy(zero_tile[:, D:D + 1], const[:, C_DUM:C_DUM + 1]).then_inc(consts_done, 1)
            def matrix_lo(i, n):
                dve.wait_ge(w_hi_done, i + 1)
                tt(w_lo[n][:, :, :], prob[:, i % 2].rearrange("p c h m -> p c (h m)"), w_hi[n][:, :, :].bitcast(f32), ALU.subtract).then_inc(w_lo_done, 1)

            matrix_lo(0, "k")
            matrix_lo(1, "q")

            def after_first():
                matrix_lo(2, "v")
                matrix_lo(3, "o")

            def hold(semaphore, value):
                dve.wait_ge(semaphore, value)
                dve.sem_inc(dve_held, 1)

            def attention_max(b, c):
                r = b.ring(2)
                if c == 0:
                    dve.wait_ge(bias_done, b.count(1, 1))
                    if isinstance(b.g, int) and 4 * b.g + b.off == 0:
                        dve.wait_ge(w_lo_done, 4)
                if b.after(2):
                    dve.wait_ge(pT_full, b.count(4, c - 7))
                hold(s_full, b.count(4, c + 1))
                for h in range(HC):
                    n = HC * c + h
                    last = nc.vector.tensor_tensor_reduce(out=prob[:, r, c, h, :], in0=ps_s[c % 2][:, P * h:P * h + P], in1=bias[:, b.ring(4), :],
                                                          scale=-1.0, scalar=BIG, op0=ALU.add, op1=ALU.min, accum_out=nmax[:, r, n:n + 1])
                last.then_inc(s_read, 1)
                dve.wait_ge(s_read, b.count(4, c + 1))
                nc.vector.tensor_reduce(amax[:, r, HC * c:HC * c + HC], prob[:, r, c, :, :], axis=AX.X, op=ALU.max,
                                        apply_absolute_value=True).then_inc(absmax_done, 1)

            def inverse_sums(b):
                r = b.ring(2)
                dve.wait_ge(exp_done, b.count(4, 4))
                if b.after(2):
                    dve.wait_ge(prob_done, b.count(4, -4))
                nc.vector.reciprocal(rinv[:, r, :], rsum[:, r, :]).then_inc(rinv_step, 1)
                dve.wait_ge(rinv_step, b.count(2, 1))
                nc.vector.scalar_tensor_tensor(out=rinv[:, r, :], in0=amax[:, r, :], scalar=0.0, in1=rinv[:, r, :],
                                               op0=ALU.not_equal, op1=ALU.mult).then_inc(rinv_step, 1)

            wide = lambda t: t[:, :].unsqueeze(2).to_broadcast([P, 2, E])
            rev = const[:, C_REV:C_REV + 2 * E].rearrange("p (a e) -> p a e", a=2)

            def choose_first(p):
                step = [0]

                def link(ins):
                    step[0] += 1
                    ins.then_inc(route_step, 1)
                    dve.wait_ge(route_step, p.count(ROUTE, step[0]))

                dve.wait_ge(gsum_full, p.count(1, 1))
                link(tt(score[:, :, :], G_S.rearrange("p (a e) -> p a e", a=2), gate_bias[:, :].unsqueeze(1).to_broadcast([P, 2, E]), ALU.add))
                link(ts(score[:, :, :], score[:, :, :], GATE_EPS, None, ALU.max))
                link(nc.vector.tensor_reduce(m1[:, :], score[:, :, :], axis=AX.X, op=ALU.max))
                link(tt(dlt[:, :, :], score[:, :, :], wide(m1), ALU.subtract))
                link(tt(eq[:, :, :], score[:, :, :], wide(m1), ALU.is_equal))
                link(tt(key[:, :, :], eq[:, :, :], rev, ALU.mult))
                link(nc.vector.tensor_reduce(kmax[:, :], key[:, :, :], axis=AX.X, op=ALU.max))
                link(tt(mask[:, 0], key[:, :, :], wide(kmax), ALU.is_equal))

            def choose_second(p):
                step = [8]

                def link(ins):
                    step[0] += 1
                    ins.then_inc(route_step, 1)
                    dve.wait_ge(route_step, p.count(ROUTE, step[0]))

                link(nc.vector.scalar_tensor_tensor(out=score2[:, :, :], in0=mask[:, 0], scalar=-BIG, in1=score[:, :, :], op0=ALU.mult, op1=ALU.add))
                link(nc.vector.tensor_reduce(m2[:, :], score2[:, :, :], axis=AX.X, op=ALU.max))
                link(tt(eq[:, :, :], score2[:, :, :], wide(m2), ALU.is_equal))
                link(tt(key[:, :, :], eq[:, :, :], rev, ALU.mult))
                link(nc.vector.tensor_reduce(kmax[:, :], key[:, :, :], axis=AX.X, op=ALU.max))
                link(tt(mask[:, 1], key[:, :, :], wide(kmax), ALU.is_equal))
                if p.after(1):
                    dve.wait_ge(place_full, p.count())
                link(tt(mask_sum[:, 0:2, :], mask[:, 0], mask[:, 1], ALU.add))

            def weigh(p):
                step = [15]

                def link(ins):
                    step[0] += 1
                    ins.then_inc(route_step, 1)
                    dve.wait_ge(route_step, p.count(ROUTE, step[0]))

                dve.wait_ge(gexp_done, p.count(1, 1))
                nc.vector.tensor_reduce(den[:, :], eexp[:, :, :], axis=AX.X, op=ALU.add)
                link(tt(em[:, :, :], eexp[:, :, :], mask[:, 1], ALU.mult))
                nc.vector.reciprocal(wgt[:, 0, :], den[:, :])
                link(nc.vector.tensor_reduce(e2[:, :], em[:, :, :], axis=AX.X, op=ALU.max))
                link(tt(wgt[:, 1, :], e2[:, :], wgt[:, 0, :], ALU.mult))
                link(ts(wgt[:, :, :], wgt[:, :, :], W_THRES, None, ALU.max))
                link(tt(wtot[:, :], wgt[:, 0, :], wgt[:, 1, :], ALU.add))
                link(nc.vector.reciprocal(wtot[:, :], wtot[:, :]))
                link(nc.vector.scalar_tensor_tensor(out=wgt[:, :, :], in0=wgt[:, :, :], scalar=1.0 / K, in1=wtot[:, :].unsqueeze(1).to_broadcast([P, K, 2]),
                                                    op0=ALU.mult, op1=ALU.mult))
                link(tt(comb_k[:, :, :, :], mask[:, :, :, :], wgt[:, :, :].unsqueeze(3).to_broadcast([P, K, 2, E]), ALU.mult))
                if p.after(2):
                    for a in range(2):
                        dve.wait_ge(scattered[a], p.count(32, -32))
                k = 2 * p.ring(2)
                tt(xn2[:, k:k + 2, D + 1:W], comb_k[:, 0], comb_k[:, 1], ALU.add)
                link(nc.vector.tensor_copy(xn2[:, k:k + 2, D], const[:, bass.ds(p.count(2, C_TOK), 2)]))

            def find_places(p):
                step = [0]

                def link(ins):
                    step[0] += 1
                    ins.then_inc(place_step, 1)
                    dve.wait_ge(place_step, p.count(PLACE, step[0]))

                r = p.ring(2)
                old, new = fill[:, r, :], fill[:, 1 - r, :]
                places = G_P.rearrange("p (a e) -> p a e", a=3)
                dve.wait_ge(place_full, p.count(1, 1))
                tt(place[:, :, :], places[:, 0:2, :], old.unsqueeze(1).to_broadcast([P, 2, E]), ALU.add)
                link(tt(new, places[:, 2, :], old, ALU.add))
                for k in range(K):
                    last = tt(place_k[:, k], place[:, :, :], mask[:, k], ALU.mult)
                link(last)
                link(nc.vector.tensor_reduce(posf[:, :, :], place_k[:, :, :, :], axis=AX.X, op=ALU.add))
                if p.after(2):
                    for a in range(2):
                        dve.wait_ge(scattered[a], p.count(32, -32))
                link(nc.vector.tensor_copy(pos[:, r], posf[:, :, :]))

            def body(g):
                for j in range(4):
                    for c in range(DC):
                        b = graph(g, j)
                        if b.valid:
                            attention_max(b, c)
                        if c == 0:
                            p = pair(g, j - 4)
                            if j % 2 and p.valid:
                                dve.wait_ge(e_hi_done, p.count(1, 1))
                                tt(e_lo[:, :], e_stage[:, :], e_hi[:, :].bitcast(f32), ALU.subtract).then_inc(e_lo_done, 1)
                            b = graph(g, j - 1)
                            if b.valid:
                                inverse_sums(b)
                            p = pair(g, j - 6)
                            if j % 2 == 0 and p.valid:
                                weigh(p)
                            b = graph(g, j - 3)
                            if b.valid:
                                dve.wait_ge(rstd2_step, b.count(RSTD, RSTD))
                                if b.after(4):
                                    q = pair(g, j - 3)
                                    dve.wait_ge(scattered[b.ring(2)], q.count(32, -32))
                                ts(xn2[:, b.ring(4), 0:D], xres[:, b.ring(2), :], mv2[:, b.ring(4), 0:1], rstd2[:, b.ring(4):b.ring(4) + 1],
                                   ALU.subtract, ALU.mult).then_inc(xn2_done, 1)
                            p = pair(g, j + 3)
                            if j % 2 and p.valid:
                                dve.wait_ge(rstd1_step, p.count(RSTD, RSTD))
                                for r in range(2):
                                    k = 2 * p.ring(2) + r
                                    ts(xin[:, k, :], xin[:, k, :], mv1[:, k, 0:1], rstd1[:, k:k + 1], ALU.subtract, ALU.mult).then_inc(xn_done, 1)
                            b = graph(g, j - 2)
                            if b.valid:
                                dve.wait_ge(oT_hi_done, b.count(1, 1))
                                tt(oT_lo[:, b.ring(2)].rearrange("p c t -> p (c t)"), ps_o[:, :],
                                   oT_hi[:, b.ring(2)].rearrange("p c t -> p (c t)").bitcast(f32), ALU.subtract).then_inc(oT_lo_done, 1)
                        if c == 1:
                            p = pair(g, j - 6)
                            if j % 2 == 0 and p.valid:
                                find_places(p)
                            b = graph(g, j + 5)
                            if b.valid:
                                k = b.ring(4)
                                dve.wait_ge(x_in[k], 16 * b.turn(4) + 16)
                                nc.vector.bn_stats(st1[:, k, :], xin[:, k, :]).then_inc(stats1, 1)
                                hold(stats1, b.count(1, 1))
                                nc.vector.bn_aggr(mv1[:, k, :], st1[:, k, :]).then_inc(mean1, 1)
                        if c == 2:
                            p = pair(g, j - 5)
                            if j % 2 and p.valid:
                                choose_first(p)
                            b = graph(g, j - 2)
                            if b.valid:
                                r, k = b.ring(2), b.ring(4)
                                dve.wait_ge(proj_full["O"], b.count(1, 1))
                                dve.wait_ge(xres_in[r], 16 * b.turn(2) + 16)
                                bank = ps_p[bank_of(j, number(j, "O"))]
                                tt(xres[:, r, :], bank[:, :], xres[:, r, :], ALU.add).then_inc(x1_done, 1)
                                dve.wait_ge(x1_done, b.count(1, 1))
                                nc.vector.bn_stats(st2[:, k, :], xres[:, r, :]).then_inc(stats2, 1)
                                hold(stats2, b.count(1, 1))
                                nc.vector.bn_aggr(mv2[:, k, :], st2[:, k, :]).then_inc(mean2, 1)
                        if c == 3:
                            p = pair(g, j - 5)
                            if j % 2 and p.valid:
                                choose_second(p)
                        if c in (1, 2):
                            p, part = pair(g, j + 3), c - 1
                            if j % 2 and p.valid:
                                r = p.ring(2)
                                dve.wait_ge(xT_hi_done, p.count(2, part + 1))
                                hi = xT_hi[:, r, 2 * part:2 * part + 2, :].rearrange("p c t -> p (c t)")
                                lo = xT_lo[:, r, 2 * part:2 * part + 2, :].rearrange("p c t -> p (c t)")
                                tt(lo, ps_p[bank_of(j, number(j, "X", part))][:, :], hi.bitcast(f32), ALU.subtract).then_inc(xT_lo_done, 1)

            turns(dve, body, after_first)
            dve.wait_ge(place_step, PLACE * (B // 2))
            nc.vector.tensor_copy(ends[:, :], fill[0:1, 0, :]).then_inc(fill_done, 1)

        @block.gpsimd
        def _(pool):
            tt, ts = nc.gpsimd.tensor_tensor, nc.gpsimd.tensor_scalar
            pool.memset(half[:, :], -0.5).then_inc(half_done, 1)
            pool.wait_ge(half_done, 1)

            def hold(semaphore, value):
                pool.wait_ge(semaphore, value)
                pool.sem_inc(pool_held, 1)

            def rstd(step_sem, base, var, nwt, out_, var_in, n):
                ops = [lambda: ts(var, var_in, LN_EPS, None, ALU.add),
                       lambda: tt(out_, var, half[:, 0:n], ALU.pow),
                       lambda: tt(nwt, var, out_, ALU.mult),
                       lambda: tt(nwt, nwt, out_, ALU.mult),
                       lambda: ts(nwt, nwt, -0.5, 1.5, ALU.mult, ALU.add),
                       lambda: tt(out_, out_, nwt, ALU.mult)]
                for i, op in enumerate(ops):
                    op().then_inc(step_sem, 1)
                    if i < len(ops) - 1:
                        hold(step_sem, base(i + 1))

            def body(g):
                for j in range(4):
                    for c in range(DC):
                        b = graph(g, j - 1)
                        if b.valid:
                            r = b.ring(2)
                            if c == 0:
                                hold(rinv_step, b.count(2, 2))
                            tt(prob[:, r, c], prob[:, r, c], rinv[:, r, HC * c:HC * c + HC].unsqueeze(2).to_broadcast([P, HC, P]), ALU.mult)\
                                .then_inc(prob_done, 1)
                        if c == 0:
                            b = graph(g, j + 1)
                            if b.valid:
                                k = b.ring(4)
                                hold(bias_in[k], 16 * b.turn(4) + 16)
                                tt(bias[:, k, :], bias[:, k, :], bias[:, k, :], ALU.add).then_inc(bias_done, 1)
                        if c == 2 and j % 2 == 0:
                            p = pair(g, j + 4)
                            if p.valid:
                                k = 2 * p.ring(2)
                                hold(mean1, p.count(2, 2))
                                if p.after(2):
                                    hold(xn_done, p.count(2, -2))
                                rstd(rstd1_step, lambda i, p=p: p.count(RSTD, i), var1[:, k:k + 2], nwt1[:, k:k + 2], rstd1[:, k:k + 2], mv1[:, k:k + 2, 1], 2)
                        if c == 3:
                            b = graph(g, j - 2)
                            if b.valid:
                                k = b.ring(4)
                                hold(mean2, b.count(1, 1))
                                rstd(rstd2_step, lambda i, b=b: b.count(RSTD, i), var2[:, k:k + 1], nwt2[:, k:k + 1], rstd2[:, k:k + 1], mv2[:, k, 1:2], 1)
                        if c >= 2 and j % 2 == 0:
                            p = pair(g, j - 6)
                            if p.valid:
                                if c == 2:
                                    hold(place_step, p.count(PLACE, PLACE))
                                    hold(route_step, p.count(ROUTE, ROUTE))
                                r, a = p.ring(2), c - 2
                                for k in range(K):
                                    pool.indirect_dma_start(out=x_lists, out_offset=bass.IndirectOffsetOnAxis(ap=pos[:, r, k, a:a + 1], axis=0),
                                                            in_=xn2[:, 2 * r + a, :], in_offset=None).then_inc(scattered[a], 16)

            turns(pool, body)
            for a in range(2):
                pool.wait_ge(scattered[a], 32 * (B // 2))


def phase_b(nc, v):
    f32, f32r, i32 = v["f32"], v["f32r"], v["i32"]
    ALU, ACT, AX = v["ALU"], v["ACT"], v["AX"]
    sem, sems = v["sem"], v["sems"]
    const, ident, fill, ends, zero_tile = v["const"], v["ident"], v["fill"], v["ends"], v["zero_tile"]
    x_lists, e_parts, out = v["x_lists"], v["e_parts"], v["out"]
    R = RING
    N = 2 * R

    mem = ExitStack()
    with mem:
        def sb(name, shape, dt=f32):
            return v["sb"](mem, name, shape, dt)

        we_hi = sb("we_hi", [P, E * DC * D], f32r)
        we_lo = sb("we_lo", [P, E * DC * D], f32r)
        e_bias = sb("e_bias", [P, E * D])
        xg = sb("xg", [P, R, W])
        xgT_hi = sb("xgT_hi", [P, R, DC, P], f32r)
        xgT_lo = sb("xgT_lo", [P, R, DC, P], f32r)
        token = sb("token", [P, N, 1], i32)
        comb = sb("comb", [P, N * E])
        yt = sb("yt", [P, R, D])
        one = sb("one", [1, E])
        n_e, past, skip = sb("n_e", [1, E]), sb("past", [1, E]), sb("skip", [1, E])
        more = sb("more", [1, E, B])
        passed = sb("passed", [1, TILES, E])
        tab_f = sb("tab_f", [1, 3, TILES])
        tab = sb("tab", [1, 3, TILES], i32)

        ps_x = [v["pb"](mem, f"ps_x{i}", [P, 512], f32) for i in range(R)]
        ps_y = [v["pb"](mem, f"ps_y{i}", [P, 512], f32) for i in range(R)]

        ebias_in, parts_in = sem("ebias_in"), sems("parts_in", E)
        experts_in, padded = sem("experts_in"), sem("padded")
        tab_step = sem("tab_step")
        xg_in, added = sems("xg_in", R), sems("added", R)
        xgT_full, xgT_hi_done, xgT_lo_done = sem("xgT_full"), sem("xgT_hi_done"), sem("xgT_lo_done")
        y_full, y_step = sem("y_full"), sem("y_step")
        meta_done, poolb_held = sem("meta_done"), sem("poolb_held")
        TAB = 15

        def tile(g, off):
            return Item(g, N, off, TILES)

        def turns(eng, body):
            body(-1)
            body(0)
            with eng.Fori(1, TILES // N - 1) as g:
                body(g)
            for g in range(TILES // N - 1, TILES // N + 2):
                body(g)

        block = mem.enter_context(nc.Block())

        @block.sync
        def _(sp):
            for e in range(E):
                for i, w in enumerate((we_hi, we_lo)):
                    sp.dma_start(w[:, e * DC * D:(e + 1) * DC * D].bitcast(f32).rearrange("p (c f) -> p c f", c=DC),
                                 e_parts[i, DC * e:DC * e + DC].rearrange("c p f -> p c f")).then_inc(parts_in[e], 16)
                if e == 0:
                    sp.wait_ge(xg_in[2], 16)
                    sp.dma_start(e_bias[:, :], v["expert_b"].rearrange("(a e) f -> a (e f)", a=1).to_broadcast([P, E * D])).then_inc(ebias_in, 16)
                sp.wait_ge(parts_in[e], 32)
                sp.sem_inc(experts_in, 1)

        @block.tensor
        def _(pe):
            pe.wait_ge(tab_step, TAB)

            def body(g):
                for j in range(N):
                    t = tile(g, j + 1)
                    if t.valid:
                        r = t.ring(R)
                        pe.wait_ge(xg_in[r], 16 * t.turn(R) + 16)
                        if t.after(R):
                            pe.wait_ge(xgT_lo_done, t.count(1, 1 - R))
                        for c in range(DC):
                            last = nc.tensor.transpose(ps_x[r][:, P * c:P * c + P], xg[:, r, P * c:P * c + P], ident)
                        last.then_inc(xgT_full, 1)
                    t = tile(g, j)
                    if t.valid:
                        r = t.ring(R)
                        e = pe.value_load(tab[0:1, 0, bass.ds(t.count(), 1)], min_val=0, max_val=E - 1)
                        pe.wait_ge(experts_in, e + 1)
                        pe.wait_ge(xgT_lo_done, t.count(1, 1))
                        if t.after(R):
                            pe.wait_ge(y_step, t.count(2, 1 - 2 * R))
                        for c in range(DC):
                            hi, lo = we_hi[:, bass.ds(e * (DC * D) + c * D, D)], we_lo[:, bass.ds(e * (DC * D) + c * D, D)]
                            nc.tensor.matmul(ps_y[r][:, :], xgT_hi[:, r, c, :], hi, start=c == 0, stop=False)
                            nc.tensor.matmul(ps_y[r][:, :], xgT_hi[:, r, c, :], lo, start=False, stop=False)
                            last = nc.tensor.matmul(ps_y[r][:, :], xgT_lo[:, r, c, :], hi, start=False, stop=c == DC - 1)
                        last.then_inc(y_full, 1)
            turns(pe, body)

        @block.scalar
        def _(act):
            for e in range(E):
                end = act.value_load(ends[0:1, e:e + 1], min_val=0, max_val=ROWS - P)
                act.dma_start(x_lists[bass.ds(end, P), :], zero_tile[:, :]).then_inc(padded, 16)
            act.wait_ge(padded, 16 * E)
            act.wait_ge(tab_step, TAB)

            def body(g):
                for j in range(N):
                    t = tile(g, j + 1)
                    if t.valid:
                        r = t.ring(R)
                        act.wait_ge(xgT_full, t.count(1, 1))
                        if t.after(R):
                            act.wait_ge(y_full, t.count(1, 1 - R))
                        nc.scalar.activation(xgT_hi[:, r].rearrange("p c t -> p (c t)"), ps_x[r][:, :], ACT.Copy).then_inc(xgT_hi_done, 1)
                    t = tile(g, j + 3)
                    if t.valid:
                        row = act.value_load(tab[0:1, 1, bass.ds(t.count(), 1)], min_val=0, max_val=ROWS - P)
                        if t.after(R):
                            act.wait_ge(xgT_full, t.count(1, 1 - R))
                            act.wait_ge(meta_done, t.count(2, 2 - 2 * R))
                        act.dma_start(xg[:, t.ring(R), :], x_lists[bass.ds(row, P), :]).then_inc(xg_in[t.ring(R)], 16)
            turns(act, body)

        @block.vector
        def _(dve):
            tt, ts = nc.vector.tensor_tensor, nc.vector.tensor_scalar
            step = [0]

            def link(ins):
                step[0] += 1
                ins.then_inc(tab_step, 1)
                dve.wait_ge(tab_step, step[0])

            across = lambda t: t[:, :].unsqueeze(1).to_broadcast([1, TILES, E])
            link(nc.vector.memset(one[:, :], 1.0))
            link(tt(n_e[:, :], fill[0:1, 0, :], const[0:1, C_BASE:C_BASE + E], ALU.subtract))
            link(tt(more[:, :, :], n_e[:, :].unsqueeze(2).to_broadcast([1, E, B]),
                    const[0:1, C_MULT:C_MULT + B].unsqueeze(1).to_broadcast([1, E, B]), ALU.is_gt))
            link(nc.vector.tensor_reduce(n_e[:, :], more[:, :, :], axis=AX.X, op=ALU.add))
            link(nc.vector.tensor_tensor_scan(past[:, :], one[:, :], n_e[:, :], 0.0, ALU.mult, ALU.add))
            link(ts(skip[:, :], n_e[:, :], -float(P), float(LIST), ALU.mult, ALU.add))
            link(tt(passed[:, :, :], const[0:1, C_TILE:C_TILE + TILES].unsqueeze(2).to_broadcast([1, TILES, E]), across(past), ALU.is_ge))
            link(nc.vector.tensor_reduce(tab_f[:, 0, :], passed[:, :, :], axis=AX.X, op=ALU.add))
            link(tt(passed[:, :, :], passed[:, :, :], across(skip), ALU.mult))
            link(nc.vector.tensor_reduce(tab_f[:, 1, :], passed[:, :, :], axis=AX.X, op=ALU.add))
            tt(tab_f[:, 2, 0:1], tab_f[:, 0, 0:1], tab_f[:, 0, 0:1], ALU.is_equal)
            link(tt(tab_f[:, 2, 1:TILES], tab_f[:, 0, 1:TILES], tab_f[:, 0, 0:TILES - 1], ALU.not_equal))
            link(tt(tab_f[:, 2, :], tab_f[:, 2, :], const[0:1, C_DEP:C_DEP + TILES], ALU.add))
            ts(tab_f[:, 2, :], tab_f[:, 2, :], 16.0, None, ALU.mult)
            link(ts(tab_f[:, 0, :], tab_f[:, 0, :], float(E - 1), None, ALU.min))
            link(nc.vector.scalar_tensor_tensor(out=tab_f[:, 1, :], in0=const[0:1, C_TILE:C_TILE + TILES], scalar=float(P), in1=tab_f[:, 1, :],
                                                op0=ALU.mult, op1=ALU.add))
            link(nc.vector.tensor_copy(tab[:, :, :], tab_f[:, :, :]))

            def body(g):
                for j in range(N):
                    t = tile(g, j + 1)
                    if t.valid:
                        r = t.ring(R)
                        dve.wait_ge(xgT_hi_done, t.count(1, 1))
                        tt(xgT_lo[:, r].rearrange("p c t -> p (c t)"), ps_x[r][:, :], xgT_hi[:, r].rearrange("p c t -> p (c t)").bitcast(f32),
                           ALU.subtract).then_inc(xgT_lo_done, 1)
                    t = tile(g, j - 1)
                    if t.valid:
                        r, m = t.ring(R), t.ring(N)
                        e = dve.value_load(tab[0:1, 0, bass.ds(t.count(), 1)], min_val=0, max_val=E - 1)
                        dve.wait_ge(y_full, t.count(1, 1))
                        if t.after(R):
                            dve.wait_ge(added[r], 16 * t.turn(R))
                        elif t.count() == 0:
                            dve.wait_ge(ebias_in, 16)
                        tt(yt[:, r, :], ps_y[r][:, :], e_bias[:, bass.ds(e * D, D)], ALU.add).then_inc(y_step, 1)
                        dve.wait_ge(meta_done, t.count(2, 2))
                        dve.wait_ge(y_step, t.count(2, 1))
                        ts(yt[:, r, :], yt[:, r, :], comb[:, bass.ds(e + E * m, 1)], None, ALU.mult).then_inc(y_step, 1)
            turns(dve, body)

        @block.gpsimd
        def _(pool):
            def hold(semaphore, value):
                pool.wait_ge(semaphore, value)
                pool.sem_inc(poolb_held, 1)

            pool.wait_ge(tab_step, TAB)

            def body(g):
                for j in range(N):
                    t = tile(g, j + 1)
                    if t.valid:
                        r, m = t.ring(R), t.ring(N)
                        hold(xg_in[r], 16 * t.turn(R) + 16)
                        if t.after(N):
                            hold(added[r], 16 * t.turn(R) - 16)
                        nc.gpsimd.tensor_copy(token[:, m, :], xg[:, r, D:D + 1]).then_inc(meta_done, 1)
                        nc.gpsimd.tensor_copy(comb[:, E * m:E * m + E], xg[:, r, D + 1:W]).then_inc(meta_done, 1)
                    t = tile(g, j - 1)
                    if t.valid:
                        r, m = t.ring(R), t.ring(N)
                        if t.after(2 * R):
                            need = pool.value_load(tab[0:1, 2, bass.ds(t.count(), 1)], min_val=16, max_val=16 * (TILES // R + 1))
                            hold(added[(j - 3) % R], 16 * tile(g, j - 3).turn(R) + 16)
                            hold(added[(j - 2) % R], need)
                        elif t.after(1):
                            pool.wait_ge(added[(j - 2) % R], 16 * tile(g, j - 2).turn(R) + 16)
                        hold(y_step, t.count(2, 2))
                        pool.indirect_dma_start(out=out, out_offset=bass.IndirectOffsetOnAxis(ap=token[:, m, :], axis=0),
                                                in_=yt[:, r, :], in_offset=None, compute_op=ALU.add).then_inc(added[r], 16)
            turns(pool, body)
            for r in range(R):
                pool.wait_ge(added[r], 16 * (TILES // R))


def constants():
    c = np.zeros((P, C_ALL), np.float32)
    c[:, C_ID:C_ID + P] = np.eye(P)
    for e in range(E):
        c[e::HD, C_SEL + e] = 1.0
    c[:, C_REV:C_REV + 2 * E] = np.tile(E - np.arange(E), 2)
    c[:, C_BASE:C_BASE + E] = LIST * np.arange(E)
    c[:, C_ROW] = np.arange(P)
    c[:, C_TRI:C_TRI + P] = np.arange(P)[:, None] < np.arange(P)[None, :]
    c[:, C_MULT:C_MULT + B] = P * np.arange(B)
    c[:, C_TILE:C_TILE + TILES] = np.arange(TILES)
    c[:, C_DEP:C_DEP + TILES] = (np.arange(TILES) - 1) // RING
    c[:, C_TOK:C_TOK + B] = P * np.arange(B) + np.arange(P)[:, None]
    c[:, C_DUM:C_DUM + E] = T + P * np.arange(E) + np.arange(P)[:, None]
    return c


def kernel(**inputs):
    import concourse.bacc as bacc
    from concourse.bass_utils import run_bass_kernel_spmd

    a = {n: np.asarray(t) for n, t in inputs.items()}
    arrays = {
        "x": a["x"], "adj": a["adj"],
        "WqT": a["L0_gnn_Wq"].T, "WkT": a["L0_gnn_Wk"].T, "WvT": a["L0_gnn_Wv"].T, "WoT": a["L0_gnn_Wo"].T,
        "gate_W": a["L0_ffn_gate_W"], "gate_b": a["L0_ffn_gate_b"],
        "expert_W": a["L0_ffn_expert_W"], "expert_b": a["L0_ffn_expert_b"],
        "consts": constants(),
    }
    arrays = {n: np.ascontiguousarray(t) for n, t in arrays.items()}
    nc = bacc.Bacc("TRN2", target_bir_lowering=False, num_devices=1)
    aps = {n: nc.dram_tensor(n, t.shape, mybir.dt.from_np(t.dtype), kind="ExternalInput").ap() for n, t in arrays.items()}
    out = nc.dram_tensor("out", (T + DUMMY, D), mybir.dt.float32, kind="ExternalOutput").ap()
    build(nc, *aps.values(), out)
    r = run_bass_kernel_spmd(nc, [arrays], core_ids=[0])
    return r.results[0]["out"][:T].reshape(B, P, D)
```

```python
import numpy as np
import concourse.bass as bass
from concourse import mybir
from contextlib import ExitStack

P = 128
B = 64
D = 512
DC = D // P
H = 16
HD = D // H
HC = P // HD
E = 8
K = 2
SCALE = float(D) ** -0.5
LN_EPS = 1e-5
GATE_EPS = 1e-4
W_THRES = 0.1
BIG = 3e38

T = B * P
LIST = T + P
TILES = T * K // P + E - 1
SPARE = (E - 1) * P
ROWS = E * LIST + SPARE
W = D + 1 + E
RING = 3
DUMMY = E * P

C_ID, C_SEL, C_REV, C_BASE, C_TRI = 0, P, P + E, P + 3 * E, P + 4 * E
C_MULT = C_TRI + P
C_TILE = C_MULT + B
C_DEP = C_TILE + TILES
C_TOK = C_DEP + TILES
C_DUM = C_TOK + B
C_ALL = C_DUM + E


class Item:

    def __init__(self, g, per, off, n):
        self.g, self.per, self.off, self.n = g, per, off, n

    @property
    def valid(self):
        return not isinstance(self.g, int) or 0 <= self.per * self.g + self.off < self.n

    def after(self, before):
        return not isinstance(self.g, int) or self.per * self.g + self.off >= before

    def count(self, m=1, t=0):
        return m * self.per * self.g + (m * self.off + t)

    def ring(self, n):
        return self.off % n

    def turn(self, n):
        return (self.per // n) * self.g + self.off // n


def build(nc, x, adj, WqT, WkT, WvT, WoT, gate_W, gate_b, expert_W, expert_b, consts, out):
    f32, f32r, bf16, i32 = mybir.dt.float32, mybir.dt.float32r, mybir.dt.bfloat16, mybir.dt.int32
    ALU, ACT, AX = mybir.AluOpType, mybir.ActivationFunctionType, mybir.AxisListType

    x_lists = nc.dram_tensor("x_lists", [ROWS, W], f32, kind="Internal").ap()
    e_parts = nc.dram_tensor("e_parts", [2, E * DC, P, D], f32, kind="Internal").ap()

    top = ExitStack()
    with top:
        def sb(stack, name, shape, dt=f32):
            return stack.enter_context(nc.sbuf_tensor(name, shape, dt))

        def pb(stack, name, shape, dt=f32):
            return stack.enter_context(nc.psum_tensor(name, shape, dt))

        def sem(name):
            return top.enter_context(nc.semaphore(name))

        def sems(name, n):
            return [sem(f"{name}{i}") for i in range(n)]

        const = sb(top, "const", [P, C_ALL])
        ident = const[:, C_ID:C_ID + P]
        fill = sb(top, "fill", [P, 2, E])
        ends = sb(top, "ends", [1, E], i32)
        tab = sb(top, "tab", [1, 3, TILES], i32)
        zero_tile = sb(top, "zero_tile", [P, W])
        const_in = sem("const_in")
        fill_done = sem("fill_done")

        phase_a(nc, locals())
        phase_b(nc, locals())


def phase_a(nc, v):
    f32, f32r, bf16, i32 = v["f32"], v["f32r"], v["bf16"], v["i32"]
    ALU, ACT, AX = v["ALU"], v["ACT"], v["AX"]
    sem, sems = v["sem"], v["sems"]
    const, ident, fill, ends, zero_tile, tab = v["const"], v["ident"], v["fill"], v["ends"], v["zero_tile"], v["tab"]
    const_in, fill_done = v["const_in"], v["fill_done"]
    x, adj, x_lists, e_parts, out = v["x"], v["adj"], v["x_lists"], v["e_parts"], v["out"]

    mem = ExitStack()
    with mem:
        def sb(name, shape, dt=f32):
            return v["sb"](mem, name, shape, dt)

        def pb(name):
            return v["pb"](mem, name, [P, 512], f32)

        w_hi = {n: sb(f"w{n}_hi", [P, DC, D], f32r) for n in "kqvo"}
        w_lo = {n: sb(f"w{n}_lo", [P, DC, D], f32r) for n in "kqvo"}
        gate_w = sb("gate_w", [P, DC, HD])
        gate_bias = sb("gate_bias", [P, E])
        tri = sb("tri", [P, P], bf16)
        ones = sb("ones", [P, P], bf16)
        half = sb("half", [P, 2])
        xin = sb("xin", [P, 4, D])
        xres = sb("xres", [P, 2, D])
        bias = sb("bias", [P, 4, P])
        xT_hi = sb("xT_hi", [P, 2, DC, 2 * P], f32r)
        xT_lo = sb("xT_lo", [P, 2, DC, 2 * P], f32r)
        qT_hi = sb("qT_hi", [P, DC, 2 * P], f32r)
        qT_lo = sb("qT_lo", [P, DC, 2 * P], f32r)
        kT = sb("kT", [P, 2, DC, 2 * P], f32r)
        kT_hi, kT_lo = kT[:, 0], kT[:, 1]
        kblk = sb("kblk", [P, 2, 2 * DC, HC * P], f32r)
        vv = sb("vv", [P, 4, D])
        prob = sb("prob", [P, 2, DC, HC, P])
        pT = sb("pT", [P, 2, HC, P])
        nmax, amax, rsum, rinv = (sb(n, [P, 2, H]) for n in ("nmax", "amax", "rsum", "rinv"))
        oT_hi = sb("oT_hi", [P, 2, DC, P], f32r)
        oT_lo = sb("oT_lo", [P, 2, DC, P], f32r)
        xn2 = sb("xn2", [P, 4, W])
        xn2T = sb("xn2T", [P, DC, 2 * P])
        st1, st2 = sb("st1", [P, 4, 6]), sb("st2", [P, 4, 6])
        mv1, mv2 = sb("mv1", [P, 4, 2]), sb("mv2", [P, 4, 2])
        var1, nwt1, rstd1 = (sb(n, [P, 4]) for n in ("var1", "nwt1", "rstd1"))
        var2, nwt2, rstd2 = (sb(n, [P, 4]) for n in ("var2", "nwt2", "rstd2"))
        gT = sb("gT", [P, 2 * P])
        score, dlt, eexp, eq, key, score2, em = (sb(n, [P, 2, E]) for n in ("score", "dlt", "eexp", "eq", "key", "score2", "em"))
        mask = sb("mask", [P, K, 2, E])
        mask_sum = sb("mask_sum", [P, 3, E], bf16)
        m1, m2, kmax, den, e2 = (sb(n, [P, 2]) for n in ("m1", "m2", "kmax", "den", "e2"))
        wgt = sb("wgt", [P, K, 2])
        wtot = sb("wtot", [P, 2])
        place = sb("place", [P, 2, E])
        place_k = sb("place_k", [P, K, 2, E])
        posf = sb("posf", [P, K, 2])
        pos = sb("pos", [P, 2, K, 2], i32)
        comb_k = sb("comb_k", [P, K, 2, E])
        spare_end = sb("spare_end", [P, E - 1, 1 + E])
        e_stage = sb("e_stage", [P, D])
        e_hi = sb("e_hi", [P, D], f32r)
        e_lo = sb("e_lo", [P, D], f32r)

        ps_s = [pb("ps_s0"), pb("ps_s1")]
        ps_t = [pb("ps_t0"), pb("ps_t1")]
        ps_o = pb("ps_o")
        ps_p = [pb("ps_p0"), pb("ps_p1")]
        ps_g = pb("ps_g")
        G_T, G_S, G_P = ps_g[:, 0:2 * P], ps_g[:, 2 * P:2 * P + 2 * E], ps_g[:, 3 * P:3 * P + 3 * E]

        stage_in = sems("stage_in", 2)
        small_in = sem("small_in")
        w_hi_done, w_lo_done = sem("w_hi_done"), sem("w_lo_done")
        zeroed, blocks_zeroed, consts_done = sem("zeroed"), sem("blocks_zeroed"), sem("consts_done")
        x_in, bias_in = sems("x_in", 4), sems("bias_in", 4)
        xres_in, x1_out = sems("xres_in", 2), sems("x1_out", 2)
        kblk_in = sems("kblk_in", 2)
        spare_out, padded, tab_step = sem("spare_out"), sem("padded"), sem("tab_step")
        e_in, e_hi_done, e_lo_done, e_out = sem("e_in"), sem("e_hi_done"), sem("e_lo_done"), sem("e_out")
        bias_done = sem("bias_done")
        stats1, mean1, rstd1_step, xn_done = sem("stats1"), sem("mean1"), sem("rstd1_step"), sem("xn_done")
        stats2, mean2, rstd2_step, xn2_done = sem("stats2"), sem("mean2"), sem("rstd2_step"), sem("xn2_done")
        proj_full = {k: sem(f"{k}_full") for k in ("K", "Q", "V", "X", "O", "X2")}
        xT_hi_done, xT_lo_done = sem("xT_hi_done"), sem("xT_lo_done")
        k_hi_done, k_lo_done, q_hi_done, q_lo_done = sem("k_hi_done"), sem("k_lo_done"), sem("q_hi_done"), sem("q_lo_done")
        v_done = sem("v_done")
        s_full, s_read, absmax_done, exp_done = sem("s_full"), sem("s_read"), sem("absmax_done"), sem("exp_done")
        rinv_step, prob_done = sem("rinv_step"), sem("prob_done")
        pT_full, pT_done, pv_done = sem("pT_full"), sem("pT_done"), sem("pv_done")
        oT_hi_done, oT_lo_done = sem("oT_hi_done"), sem("oT_lo_done")
        x1_done, xn2T_done = sem("x1_done"), sem("xn2T_done")
        gate_full, gT_done, gsum_full, gexp_done = sem("gate_full"), sem("gT_done"), sem("gsum_full"), sem("gexp_done")
        route_step, place_full, place_step = sem("route_step"), sem("place_full"), sem("place_step")
        scattered = sems("scattered", 2)
        half_done = sem("half_done")
        pool_held = sem("pool_held")
        dve_held, sp_held = sem("dve_held"), sem("sp_held")

        def graph(g, off):
            return Item(g, 4, off, B)

        def pair(g, off):
            return Item(g, 2, off // 2, B // 2)

        QUARTERS = ([[("Q", 0, 1)], [("X2", -3, 0), ("O", -2, 0)], [("K", 2, 0)], [("K", 2, 1)]],
                    [[("V", 1, 0)], [("X", 3, 0), ("O", -2, 0)], [("X", 3, 1), ("Q", 1, 0)], [("X2", -3, 0), ("V", 1, 1)]])
        EVEN, ODD = (sum(q, []) for q in QUARTERS)

        def uses(j, c):
            before = sum(len(q) for q in QUARTERS[j % 2][:c])
            return list(range(before, before + len(QUARTERS[j % 2][c])))

        def number(j, kind, part=0):
            return [(k, p) for k, _, p in (ODD if j % 2 else EVEN)].index((kind, part))

        PER = len(EVEN) + len(ODD)
        READ_BY = {"K": k_lo_done, "Q": q_lo_done, "V": v_done, "X": xT_lo_done, "O": x1_done, "X2": xn2T_done}

        def use(g, j, n):
            kind, lag, part = (ODD if j % 2 else EVEN)[n]
            if kind in ("O", "X2"):
                it = graph(g, j + lag)
                return kind, it, part, it.count(1, 1)
            it = pair(g, j + lag)
            return kind, it, part, it.count(2, part + 1)

        def bank_of(j, n):
            return (n + (len(EVEN) if j % 2 else 0)) % 2

        def bank_free(g, j, n):
            jj, nn = j, n
            for _ in range(4 * PER):
                nn -= 1
                if nn < 0:
                    jj -= 1
                    nn = len(ODD if jj % 2 else EVEN) - 1
                if bank_of(jj, nn) != bank_of(j, n):
                    continue
                kind, it, part, count = use(g, jj, nn)
                if it.valid:
                    return READ_BY[kind], count
            return None

        FIRST, LAST = -2, 17
        LOOP = (3, 14)

        def turns(eng, body):
            for g in range(FIRST, LOOP[0]):
                body(g)
            with eng.Fori(LOOP[0], LOOP[1]) as g:
                body(g)
            for g in range(LOOP[1], LAST + 1):
                body(g)

        def at(g, j, slot):
            return isinstance(g, int) and 4 * g + j == slot

        matrix = {n: w.rearrange("(c p) o -> p c o", p=P) for n, w in
                (("k", v["WkT"]), ("q", v["WqT"]), ("v", v["WvT"]), ("o", v["WoT"]))}

        def stage(i):
            return prob[:, i % 2].rearrange("p c h m -> p c (h m)")

        RSTD, ROUTE, PLACE = 6, 24, 4

        block = mem.enter_context(nc.Block())

        @block.sync
        def _(sp):
            sp.dma_start(const[:, :], v["consts"]).then_inc(const_in, 16)
            sp.wait_ge(zeroed, 1)
            sp.dma_start(gate_w[:, :, 0:E], v["gate_W"].rearrange("(c p) e -> p c e", p=P)).then_inc(small_in, 16)
            sp.dma_start(gate_bias[:, :], v["gate_b"].rearrange("(a e) -> a e", a=1).to_broadcast([P, E])).then_inc(small_in, 16)
            def hold(semaphore, value):
                sp.wait_ge(semaphore, value)
                sp.sem_inc(sp_held, 1)

            def body(g):
                for j in range(4):
                    b = graph(g, j + 1)
                    if b.valid:
                        if at(g, j, -1):
                            sp.wait_ge(blocks_zeroed, 2)
                        hold(k_lo_done, pair(g, j + 1).count(2, 2))
                        if b.after(2):
                            hold(s_full, b.count(4, -4))
                        r = b.ring(2)
                        for h in range(HC):
                            rows = slice(HD * h, HD * h + HD)
                            sp.dma_start(kblk[rows, r, :, P * h:P * h + P].bitcast(f32),
                                         kT[rows, :, :, P * r:P * r + P].rearrange("p a c t -> p (a c) t").bitcast(f32)).then_inc(kblk_in[r], 16)
                    b = graph(g, j + 6)
                    if b.valid:
                        if b.after(4):
                            hold(proj_full["X"], pair(g, j + 6).count(2, -2))
                        sp.dma_start(xin[:, b.ring(4), :], x[bass.ds(b.count(), 1)].rearrange("a p d -> (a p) d")).then_inc(x_in[b.ring(4)], 16)
                    if at(g, j, -5):
                        for i, n in ((0, "k"), (1, "q")):
                            sp.dma_start(stage(i), matrix[n]).then_inc(stage_in[i % 2], 16)
                    b = graph(g, j + 2)
                    if b.valid:
                        if b.after(4):
                            hold(s_read, b.count(4, -12))
                        sp.dma_start(bias[:, b.ring(4), :], adj[bass.ds(b.count(), 1)].rearrange("a p d -> (a p) d")).then_inc(bias_in[b.ring(4)], 16)
                    b = graph(g, j - 3)
                    if b.valid:
                        hold(x1_done, b.count(1, 1))
                        sp.dma_start(out[bass.ds(b.count(P), P), :], xres[:, b.ring(2), :]).then_inc(x1_out[b.ring(2)], 16)
                    p = pair(g, j - 6)
                    if p.valid and j % 2 == 0:
                        hold(e_lo_done, p.count(1, 1))
                        for i, part in enumerate((e_hi, e_lo)):
                            sp.dma_start(e_parts[i, bass.ds(p.count(), 1)].rearrange("a p d -> (a p) d"), part[:, :].bitcast(f32)).then_inc(e_out, 16)
                    p = pair(g, j - 4)
                    if p.valid and j % 2 == 0:
                        sp.dma_start(e_stage[:, :], v["expert_W"].rearrange("e d f -> (e d) f")[bass.ds(p.count(P), P), :]).then_inc(e_in, 16)
                    b = graph(g, j - 1)
                    if b.valid:
                        if b.after(2):
                            hold(xn2_done, b.count(1, -1))
                            hold(x1_out[b.ring(2)], 16 * b.turn(2))
                        sp.dma_start(xres[:, b.ring(2), :], x[bass.ds(b.count(), 1)].rearrange("a p d -> (a p) d")).then_inc(xres_in[b.ring(2)], 16)

            turns(sp, body)
            sp.wait_ge(fill_done, 1)
            sp.wait_ge(spare_out, 48)
            for e in range(E):
                end = sp.value_load(ends[0:1, e:e + 1], min_val=0, max_val=ROWS - P)
                sp.dma_start(x_lists[bass.ds(end, P), :], zero_tile[:, :]).then_inc(padded, 16)
            sp.wait_ge(padded, 16 * E)
            sp.wait_ge(e_out, 32 * E * DC)
            for r in range(2):
                sp.wait_ge(x1_out[r], 16 * (B // 2))

        @block.tensor
        def _(pe):
            mm = nc.tensor.matmul

            def three(out_, lhs_hi, lhs_lo, rhs_hi, rhs_lo, first, last):
                mm(out_, lhs_hi, rhs_hi, start=first, stop=False)
                mm(out_, lhs_hi, rhs_lo, start=False, stop=False)
                return mm(out_, lhs_lo, rhs_hi, start=False, stop=last)

            def wait_bank(g, j, n):
                free = bank_free(g, j, n)
                if free:
                    pe.wait_ge(*free)

            def work(g, j, n):
                kind, it, part, count = use(g, j, n)
                if not it.valid:
                    return
                bank = ps_p[bank_of(j, n)]
                if kind in ("K", "Q"):
                    pe.wait_ge(xT_lo_done, it.count(2, 2))
                    if isinstance(g, int) and 2 * g + it.off == 0:
                        pe.wait_ge(w_lo_done, 1 if kind == "K" else 2)
                    wait_bank(g, j, n)
                    r, w = it.ring(2), kind.lower()
                    for oc in range(2):
                        o = P * (2 * part + oc)
                        for c in range(DC):
                            last = three(bank[:, 2 * P * oc:2 * P * oc + 2 * P], w_hi[w][:, c, o:o + P], w_lo[w][:, c, o:o + P],
                                         xT_hi[:, r, c, :], xT_lo[:, r, c, :], c == 0, c == DC - 1)
                elif kind == "V":
                    if isinstance(g, int) and 2 * g + it.off == 0:
                        pe.wait_ge(w_lo_done, 3)
                    wait_bank(g, j, n)
                    r, t = it.ring(2), slice(P * part, P * part + P)
                    for c in range(DC):
                        last = three(bank[:, :], xT_hi[:, r, c, t], xT_lo[:, r, c, t], w_hi["v"][:, c, :], w_lo["v"][:, c, :], c == 0, c == DC - 1)
                elif kind == "O":
                    pe.wait_ge(oT_lo_done, it.count(1, 1))
                    if isinstance(g, int) and 4 * g + it.off == 0:
                        pe.wait_ge(w_lo_done, 4)
                    wait_bank(g, j, n)
                    r = it.ring(2)
                    for c in range(DC):
                        last = three(bank[:, :], oT_hi[:, r, c, :], oT_lo[:, r, c, :], w_hi["o"][:, c, :], w_lo["o"][:, c, :], c == 0, c == DC - 1)
                elif kind == "X":
                    pe.wait_ge(xn_done, it.count(2, 2))
                    wait_bank(g, j, n)
                    for cc in range(2):
                        c = 2 * part + cc
                        for r in range(2):
                            last = nc.tensor.transpose(bank[:, P * (2 * cc + r):P * (2 * cc + r) + P],
                                                       xin[:, 2 * it.ring(2) + r, P * c:P * c + P], ident)
                else:
                    pe.wait_ge(xn2_done, it.count(1, 1))
                    wait_bank(g, j, n)
                    for c in range(DC):
                        last = nc.tensor.transpose(bank[:, P * c:P * c + P], xn2[:, it.ring(4), P * c:P * c + P], ident)
                last.then_inc(proj_full[kind], 1)

            def scores(b, p, c):
                if c == 0:
                    pe.wait_ge(kblk_in[b.ring(2)], 64 * b.turn(2) + 64)
                if c % 2 == 0:
                    pe.wait_ge(q_lo_done, p.count(2, c // 2 + 1))
                if b.after(1) or c >= 2:
                    pe.wait_ge(s_read, b.count(4, c - 1))
                r, t = b.ring(2), slice(P * b.ring(2), P * b.ring(2) + P)
                three(ps_s[c % 2][:, :], qT_hi[:, c, t], qT_lo[:, c, t], kblk[:, r, c, :], kblk[:, r, DC + c, :], True, True).then_inc(s_full, 1)

            def transpose_probs(b, c):
                pe.wait_ge(prob_done, b.count(4, c + 1))
                if b.after(1) or c >= 2:
                    pe.wait_ge(pT_done, b.count(4, c - 1))
                for h in range(HC):
                    last = nc.tensor.transpose(ps_t[c % 2][:, P * h:P * h + P], prob[:, b.ring(2), c, h, :], ident)
                last.then_inc(pT_full, 1)

            def times_v(b, c):
                pe.wait_ge(pT_done, b.count(4, c + 1))
                if c == 0:
                    pe.wait_ge(v_done, b.count(1, 1))
                    if b.after(1):
                        pe.wait_ge(oT_lo_done, b.count(1, 0))
                for h in range(HC):
                    last = mm(ps_o[HD * h:HD * h + HD, P * c:P * c + P], vv[:, b.ring(4), HD * (HC * c + h):HD * (HC * c + h) + HD],
                              pT[:, c % 2, h, :], start=True, stop=True)
                last.then_inc(pv_done, 1)

            def attend(g, j, c):
                b = graph(g, j - 1 if c else j - 2)
                if b.valid:
                    times_v(b, (c - 1) % DC)

            pe.wait_ge(const_in, 16)

            def body(g):
                for j in range(4):
                    for c in range(DC):
                        b = graph(g, j)
                        if b.valid:
                            scores(b, pair(g, j), c)
                        for n in uses(j, c):
                            work(g, j, n)
                        attend(g, j, c)
                        if c == 3 and j % 2 == 0:
                            p = pair(g, j - 4)
                            if p.valid:
                                pe.wait_ge(xn2T_done, p.count(2, 2))
                                if isinstance(g, int) and 2 * g + p.off == 0:
                                    pe.wait_ge(small_in, 32)
                                if p.after(1):
                                    pe.wait_ge(place_step, p.count(PLACE, -PLACE + 1))
                                for cc in range(DC):
                                    last = mm(ps_g[HD * cc:HD * cc + HD, 0:2 * P], gate_w[:, cc, :], xn2T[:, cc, :], start=True, stop=True)
                                last.then_inc(gate_full, 1)
                        if c == 1 and j % 2:
                            p = pair(g, j - 5)
                            if p.valid:
                                pe.wait_ge(gT_done, p.count(1, 1))
                                for r in range(2):
                                    last = mm(G_S[:, E * r:E * r + E], gT[:, P * r:P * r + P], const[:, C_SEL:C_SEL + E], start=True, stop=True)
                                last.then_inc(gsum_full, 1)
                        if c == 0 and j % 2 == 0:
                            p = pair(g, j - 6)
                            if p.valid:
                                pe.wait_ge(route_step, p.count(ROUTE, 15))
                                if isinstance(g, int) and 2 * g + p.off == 0:
                                    pe.wait_ge(consts_done, 3)
                                mm(G_P, tri[:, :], mask_sum[:, :, :].rearrange("p a e -> p (a e)"), start=True, stop=False)
                                mm(G_P[:, E:3 * E], ones[:, :], mask_sum[:, 0:2, :].rearrange("p a e -> p (a e)"), start=False, stop=False)
                                mm(G_P[:, 2 * E:3 * E], ones[:, :], mask_sum[:, 0, :], start=False, stop=True).then_inc(place_full, 1)
                        b = graph(g, j - 1)
                        if b.valid:
                            transpose_probs(b, c)

            turns(pe, body)

        @block.scalar
        def _(act):
            def matrix_hi(i, n):
                act.wait_ge(stage_in[i % 2], 16 * (i // 2) + 16)
                nc.scalar.activation(w_hi[n][:, :, :], stage(i), ACT.Copy).then_inc(w_hi_done, 1)

            def rows_for_nobody():
                act.wait_ge(zeroed, 2)
                act.wait_ge(consts_done, 6)
                spare = x_lists[E * LIST:ROWS, :].rearrange("(n p) d -> p n d", p=P)
                act.dma_start(spare[:, :, 0:D], zero_tile[:, 0:D].unsqueeze(1).to_broadcast([P, E - 1, D])).then_inc(spare_out, 16)
                act.dma_start(spare[:, :, D:W], spare_end[:, :, :]).then_inc(spare_out, 16)
                act.dma_start(out[T:T + DUMMY, :].rearrange("(n p) d -> p n d", p=P), zero_tile[:, 0:D].unsqueeze(1).to_broadcast([P, E, D])).then_inc(spare_out, 16)

            matrix_hi(0, "k")
            matrix_hi(1, "q")

            def read(g, j, n):
                kind, it, part, count = use(g, j, n)
                if not it.valid or kind == "O":
                    return
                bank = ps_p[bank_of(j, n)]
                act.wait_ge(proj_full[kind], count)
                r = it.ring(2)
                if kind == "K":
                    if it.after(1):
                        for k in range(2):
                            act.wait_ge(kblk_in[k], it.count(64))
                    nc.scalar.activation(kT_hi[:, 2 * part:2 * part + 2, :].rearrange("p c t -> p (c t)"), bank[:, :], ACT.Copy).then_inc(k_hi_done, 1)
                elif kind == "Q":
                    if it.after(1):
                        act.wait_ge(s_full, it.count(8, 2 * part - 2))
                    nc.scalar.activation(qT_hi[:, 2 * part:2 * part + 2, :].rearrange("p c t -> p (c t)"), bank[:, :], ACT.Copy, scale=SCALE).then_inc(q_hi_done, 1)
                elif kind == "V":
                    if it.after(2):
                        act.wait_ge(pv_done, it.count(8, 4 * part - 12))
                    nc.scalar.activation(vv[:, 2 * r + part, :], bank[:, :], ACT.Copy).then_inc(v_done, 1)
                elif kind == "X":
                    if it.after(2):
                        act.wait_ge(proj_full["Q"], it.count(2, -2))
                    nc.scalar.activation(xT_hi[:, r, 2 * part:2 * part + 2, :].rearrange("p c t -> p (c t)"), bank[:, :], ACT.Copy).then_inc(xT_hi_done, 1)
                else:
                    p = pair(g, j - 3)
                    if p.after(1):
                        act.wait_ge(gate_full, p.count())
                    r = it.ring(2)
                    nc.scalar.activation(xn2T[:, :, P * r:P * r + P], bank[:, :].rearrange("p (c t) -> p c t", c=DC), ACT.Copy).then_inc(xn2T_done, 1)

            def exponentials(b, c, heads):
                if not b.valid:
                    return
                r = b.ring(2)
                if heads[0] == 0:
                    act.wait_ge(absmax_done, b.count(4, c + 1))
                    if b.after(2) and c == 0:
                        act.wait_ge(rinv_step, b.count(4, -4))
                for h in heads:
                    n = HC * c + h
                    last = nc.scalar.activation(prob[:, r, c, h, :], prob[:, r, c, h, :], ACT.Exp, bias=nmax[:, r, n:n + 1],
                                                scale=-1.0, accum_out=rsum[:, r, n:n + 1])
                if heads[-1] == HC - 1:
                    last.then_inc(exp_done, 1)

            def body(g):
                for j in range(4):
                    p = pair(g, j - 4)
                    if p.valid and j % 2:
                        act.wait_ge(e_in, p.count(16, 16))
                        if p.after(1):
                            act.wait_ge(e_out, p.count(32))
                        nc.scalar.activation(e_hi[:, :], e_stage[:, :], ACT.Copy).then_inc(e_hi_done, 1)
                    for c in range(DC):
                        for n in uses(j, c)[:-1]:
                            read(g, j, n)
                        exponentials(graph(g, j), c, range(0, HC // 2))
                        if c == 0:
                            b = graph(g, j - 2)
                            if b.valid:
                                act.wait_ge(pv_done, b.count(4, 4))
                                if b.after(2):
                                    act.wait_ge(proj_full["O"], b.count(1, -1))
                                nc.scalar.activation(oT_hi[:, b.ring(2)].rearrange("p c t -> p (c t)"), ps_o[:, :], ACT.Copy).then_inc(oT_hi_done, 1)
                        read(g, j, uses(j, c)[-1])
                        exponentials(graph(g, j), c, range(HC // 2, HC))
                        if c == 0 and j % 2:
                            p = pair(g, j - 5)
                            if p.valid:
                                act.wait_ge(gate_full, p.count(1, 1))
                                if p.after(1):
                                    act.wait_ge(gsum_full, p.count())
                                nc.scalar.activation(gT[:, :], G_T, ACT.Copy).then_inc(gT_done, 1)
                        if at(g, j, -3) and c == 0:
                            for i, n in ((2, "v"), (3, "o")):
                                act.wait_ge(w_lo_done, i - 1)
                                act.dma_start(stage(i), matrix[n]).then_inc(stage_in[i % 2], 16)
                        if at(g, j, -3) and c == 3:
                            matrix_hi(2, "v")
                        if at(g, j, -2) and c == 0:
                            matrix_hi(3, "o")
                        if at(g, j, -1) and c == 0:
                            rows_for_nobody()
                        if c == 3 and j % 2:
                            p = pair(g, j - 5)
                            if p.valid:
                                act.wait_ge(route_step, p.count(ROUTE, 4))
                                if p.after(1):
                                    act.wait_ge(route_step, p.count(ROUTE))
                                nc.scalar.activation(eexp[:, :, :], dlt[:, :, :], ACT.Exp).then_inc(gexp_done, 1)
                        b = graph(g, j - 1)
                        if b.valid:
                            act.wait_ge(pT_full, b.count(4, c + 1))
                            if b.after(1) or c >= 2:
                                act.wait_ge(pv_done, b.count(4, c - 1))
                            nc.scalar.activation(pT[:, c % 2].rearrange("p h t -> p (h t)"), ps_t[c % 2][:, :], ACT.Copy).then_inc(pT_done, 1)

            turns(act, body)

        @block.vector
        def _(dve):
            tt, ts = nc.vector.tensor_tensor, nc.vector.tensor_scalar
            nc.vector.memset(gate_w[:, :, :], 0.0).then_inc(zeroed, 1)
            nc.vector.memset(zero_tile[:, :], 0.0).then_inc(zeroed, 1)
            nc.vector.memset(mask_sum[:, :, :], 0.0).then_inc(consts_done, 1)
            nc.vector.memset(ones[:, :], 1.0).then_inc(consts_done, 1)
            dve.wait_ge(const_in, 16)
            nc.vector.tensor_copy(tri[:, :], const[:, C_TRI:C_TRI + P]).then_inc(consts_done, 1)
            nc.vector.tensor_copy(fill[:, 0, :], const[:, C_BASE:C_BASE + E]).then_inc(consts_done, 1)
            nc.vector.memset(spare_end[:, :, 1:1 + E], 0.0).then_inc(consts_done, 1)
            nc.vector.tensor_copy(spare_end[:, :, 0], const[:, C_DUM + 1:C_DUM + E]).then_inc(consts_done, 1)
            dve.wait_ge(zeroed, 2)
            nc.vector.tensor_copy(zero_tile[:, D:D + 1], const[:, C_DUM:C_DUM + 1]).then_inc(consts_done, 1)
            def matrix_lo(i, n):
                dve.wait_ge(w_hi_done, i + 1)
                tt(w_lo[n][:, :, :], stage(i), w_hi[n][:, :, :].bitcast(f32), ALU.subtract).then_inc(w_lo_done, 1)


            def hold(semaphore, value):
                dve.wait_ge(semaphore, value)
                dve.sem_inc(dve_held, 1)

            def low_part(g, j, n):
                kind, it, part, count = use(g, j, n)
                if not it.valid or kind not in "XKQ":
                    return
                bank = ps_p[bank_of(j, n)]
                of = lambda t: t[:, 2 * part:2 * part + 2, :].rearrange("p c t -> p (c t)")
                if kind == "X":
                    r = it.ring(2)
                    dve.wait_ge(xT_hi_done, count)
                    tt(of(xT_lo[:, r]), bank[:, :], of(xT_hi[:, r]).bitcast(f32), ALU.subtract).then_inc(xT_lo_done, 1)
                elif kind == "K":
                    dve.wait_ge(k_hi_done, count)
                    tt(of(kT_lo), bank[:, :], of(kT_hi).bitcast(f32), ALU.subtract).then_inc(k_lo_done, 1)
                else:
                    dve.wait_ge(q_hi_done, count)
                    nc.vector.scalar_tensor_tensor(out=of(qT_lo), in0=bank[:, :], scalar=SCALE, in1=of(qT_hi).bitcast(f32),
                                                   op0=ALU.mult, op1=ALU.subtract).then_inc(q_lo_done, 1)

            def attention_max(b, c):
                if not b.valid:
                    return
                r = b.ring(2)
                if c == 0:
                    dve.wait_ge(bias_done, b.count(1, 1))
                    if isinstance(b.g, int) and 4 * b.g + b.off == 0:
                        dve.wait_ge(w_lo_done, 4)
                if b.after(2):
                    dve.wait_ge(pT_full, b.count(4, c - 7))
                hold(s_full, b.count(4, c + 1))
                for h in range(HC):
                    n = HC * c + h
                    last = nc.vector.tensor_tensor_reduce(out=prob[:, r, c, h, :], in0=ps_s[c % 2][:, P * h:P * h + P], in1=bias[:, b.ring(4), :],
                                                          scale=-1.0, scalar=BIG, op0=ALU.add, op1=ALU.min, accum_out=nmax[:, r, n:n + 1])
                last.then_inc(s_read, 1)
                dve.wait_ge(s_read, b.count(4, c + 1))
                nc.vector.tensor_reduce(amax[:, r, HC * c:HC * c + HC], prob[:, r, c, :, :], axis=AX.X, op=ALU.max,
                                        apply_absolute_value=True).then_inc(absmax_done, 1)

            def first_stats(b):
                if not b.valid:
                    return
                k = b.ring(4)
                dve.wait_ge(x_in[k], 16 * b.turn(4) + 16)
                nc.vector.bn_stats(st1[:, k, :], xin[:, k, :]).then_inc(stats1, 1)
                hold(stats1, b.count(1, 1))
                nc.vector.bn_aggr(mv1[:, k, :], st1[:, k, :]).then_inc(mean1, 1)

            def inverse_sums(b, half):
                if not b.valid:
                    return
                r, heads = b.ring(2), slice(H // 2 * half, H // 2 * half + H // 2)
                dve.wait_ge(exp_done, b.count(4, 2 * half + 2))
                if b.after(2):
                    dve.wait_ge(prob_done, b.count(4, -4))
                nc.vector.reciprocal(rinv[:, r, heads], rsum[:, r, heads]).then_inc(rinv_step, 1)
                dve.wait_ge(rinv_step, b.count(4, 2 * half + 1))
                nc.vector.scalar_tensor_tensor(out=rinv[:, r, heads], in0=amax[:, r, heads], scalar=0.0, in1=rinv[:, r, heads],
                                               op0=ALU.not_equal, op1=ALU.mult).then_inc(rinv_step, 1)

            wide = lambda t: t[:, :].unsqueeze(2).to_broadcast([P, 2, E])
            rev = const[:, C_REV:C_REV + 2 * E].rearrange("p (a e) -> p a e", a=2)

            def gate_scores(p):
                step = [0]

                def link(ins):
                    step[0] += 1
                    ins.then_inc(route_step, 1)
                    dve.wait_ge(route_step, p.count(ROUTE, step[0]))

                dve.wait_ge(gsum_full, p.count(1, 1))
                link(tt(score[:, :, :], G_S.rearrange("p (a e) -> p a e", a=2), gate_bias[:, :].unsqueeze(1).to_broadcast([P, 2, E]), ALU.add))
                link(ts(score[:, :, :], score[:, :, :], GATE_EPS, None, ALU.max))
                link(nc.vector.tensor_reduce(m1[:, :], score[:, :, :], axis=AX.X, op=ALU.max))
                link(tt(dlt[:, :, :], score[:, :, :], wide(m1), ALU.subtract))

            def choose(p):
                step = [4]

                def link(ins):
                    step[0] += 1
                    ins.then_inc(route_step, 1)
                    dve.wait_ge(route_step, p.count(ROUTE, step[0]))

                link(tt(eq[:, :, :], score[:, :, :], wide(m1), ALU.is_equal))
                link(tt(key[:, :, :], eq[:, :, :], rev, ALU.mult))
                link(nc.vector.tensor_reduce(kmax[:, :], key[:, :, :], axis=AX.X, op=ALU.max))
                link(tt(mask[:, 0], key[:, :, :], wide(kmax), ALU.is_equal))
                link(nc.vector.scalar_tensor_tensor(out=score2[:, :, :], in0=mask[:, 0], scalar=-BIG, in1=score[:, :, :], op0=ALU.mult, op1=ALU.add))
                link(nc.vector.tensor_reduce(m2[:, :], score2[:, :, :], axis=AX.X, op=ALU.max))
                link(tt(eq[:, :, :], score2[:, :, :], wide(m2), ALU.is_equal))
                link(tt(key[:, :, :], eq[:, :, :], rev, ALU.mult))
                link(nc.vector.tensor_reduce(kmax[:, :], key[:, :, :], axis=AX.X, op=ALU.max))
                link(tt(mask[:, 1], key[:, :, :], wide(kmax), ALU.is_equal))
                if p.after(1):
                    dve.wait_ge(place_full, p.count())
                link(tt(mask_sum[:, 0:2, :], mask[:, 0], mask[:, 1], ALU.add))

            def weigh(p):
                step = [15]

                def link(ins):
                    step[0] += 1
                    ins.then_inc(route_step, 1)
                    dve.wait_ge(route_step, p.count(ROUTE, step[0]))

                dve.wait_ge(gexp_done, p.count(1, 1))
                nc.vector.tensor_reduce(den[:, :], eexp[:, :, :], axis=AX.X, op=ALU.add)
                link(tt(em[:, :, :], eexp[:, :, :], mask[:, 1], ALU.mult))
                nc.vector.reciprocal(wgt[:, 0, :], den[:, :])
                link(nc.vector.tensor_reduce(e2[:, :], em[:, :, :], axis=AX.X, op=ALU.max))
                link(tt(wgt[:, 1, :], e2[:, :], wgt[:, 0, :], ALU.mult))
                link(ts(wgt[:, :, :], wgt[:, :, :], W_THRES, None, ALU.max))
                link(tt(wtot[:, :], wgt[:, 0, :], wgt[:, 1, :], ALU.add))
                link(nc.vector.reciprocal(wtot[:, :], wtot[:, :]))
                link(nc.vector.scalar_tensor_tensor(out=wgt[:, :, :], in0=wgt[:, :, :], scalar=1.0 / K, in1=wtot[:, :].unsqueeze(1).to_broadcast([P, K, 2]),
                                                    op0=ALU.mult, op1=ALU.mult))
                link(tt(comb_k[:, :, :, :], mask[:, :, :, :], wgt[:, :, :].unsqueeze(3).to_broadcast([P, K, 2, E]), ALU.mult))
                if p.after(2):
                    for a in range(2):
                        dve.wait_ge(scattered[a], p.count(32, -32))
                k = 2 * p.ring(2)
                tt(xn2[:, k:k + 2, D + 1:W], comb_k[:, 0], comb_k[:, 1], ALU.add)
                link(nc.vector.tensor_copy(xn2[:, k:k + 2, D], const[:, bass.ds(p.count(2, C_TOK), 2)]))

            def find_places(p):
                step = [0]

                def link(ins):
                    step[0] += 1
                    ins.then_inc(place_step, 1)
                    dve.wait_ge(place_step, p.count(PLACE, step[0]))

                r = p.ring(2)
                old, new = fill[:, r, :], fill[:, 1 - r, :]
                places = G_P.rearrange("p (a e) -> p a e", a=3)
                dve.wait_ge(place_full, p.count(1, 1))
                tt(place[:, :, :], places[:, 0:2, :], old.unsqueeze(1).to_broadcast([P, 2, E]), ALU.add)
                link(tt(new, places[:, 2, :], old, ALU.add))
                for k in range(K):
                    last = tt(place_k[:, k], place[:, :, :], mask[:, k], ALU.mult)
                link(last)
                link(nc.vector.tensor_reduce(posf[:, :, :], place_k[:, :, :, :], axis=AX.X, op=ALU.add))
                if p.after(2):
                    for a in range(2):
                        dve.wait_ge(scattered[a], p.count(32, -32))
                link(nc.vector.tensor_copy(pos[:, r], posf[:, :, :]))

            def body(g):
                for j in range(4):
                    for c in range(DC):
                        attention_max(graph(g, j), c)
                        if c == 0:
                            inverse_sums(graph(g, j - 1), 1)
                        if c == 3:
                            inverse_sums(graph(g, j), 0)
                        for n in uses(j, c)[:-1]:
                            low_part(g, j, n)
                        if c == 0:
                            b = graph(g, j - 3)
                            if b.valid:
                                dve.wait_ge(rstd2_step, b.count(RSTD, RSTD))
                                if b.after(4):
                                    q = pair(g, j - 3)
                                    dve.wait_ge(scattered[b.ring(2)], q.count(32, -32))
                                ts(xn2[:, b.ring(4), 0:D], xres[:, b.ring(2), :], mv2[:, b.ring(4), 0:1], rstd2[:, b.ring(4):b.ring(4) + 1],
                                   ALU.subtract, ALU.mult).then_inc(xn2_done, 1)
                            p = pair(g, j + 3)
                            if j % 2 and p.valid:
                                dve.wait_ge(rstd1_step, p.count(RSTD, RSTD))
                                for r in range(2):
                                    k = 2 * p.ring(2) + r
                                    ts(xin[:, k, :], xin[:, k, :], mv1[:, k, 0:1], rstd1[:, k:k + 1], ALU.subtract, ALU.mult).then_inc(xn_done, 1)
                            b = graph(g, j - 2)
                            if b.valid:
                                dve.wait_ge(oT_hi_done, b.count(1, 1))
                                tt(oT_lo[:, b.ring(2)].rearrange("p c t -> p (c t)"), ps_o[:, :],
                                   oT_hi[:, b.ring(2)].rearrange("p c t -> p (c t)").bitcast(f32), ALU.subtract).then_inc(oT_lo_done, 1)
                        if at(g, j, -3) and c == 0:
                            matrix_lo(0, "k")
                            matrix_lo(1, "q")
                        if at(g, j, -2) and c == 0:
                            matrix_lo(2, "v")
                            matrix_lo(3, "o")
                        if c == 1:
                            p = pair(g, j - 6)
                            if j % 2 == 0 and p.valid:
                                weigh(p)
                            b = graph(g, j - 2)
                            if b.valid:
                                r, k = b.ring(2), b.ring(4)
                                dve.wait_ge(proj_full["O"], b.count(1, 1))
                                dve.wait_ge(xres_in[r], 16 * b.turn(2) + 16)
                                bank = ps_p[bank_of(j, number(j, "O"))]
                                tt(xres[:, r, :], bank[:, :], xres[:, r, :], ALU.add).then_inc(x1_done, 1)
                                dve.wait_ge(x1_done, b.count(1, 1))
                                nc.vector.bn_stats(st2[:, k, :], xres[:, r, :]).then_inc(stats2, 1)
                                hold(stats2, b.count(1, 1))
                                nc.vector.bn_aggr(mv2[:, k, :], st2[:, k, :]).then_inc(mean2, 1)
                        p = pair(g, j - 6)
                        if c == 2 and j % 2 == 0 and p.valid:
                            find_places(p)
                        if c >= 2 and j % 2 == 0:
                            first_stats(graph(g, j + 2 + c))
                        low_part(g, j, uses(j, c)[-1])
                        p = pair(g, j - 5)
                        if j % 2 and p.valid:
                            if c == 2:
                                gate_scores(p)
                            if c == 3:
                                choose(p)

            turns(dve, body)
            dve.wait_ge(place_step, PLACE * (B // 2))
            nc.vector.tensor_copy(ends[:, :], fill[0:1, 0, :]).then_inc(fill_done, 1)
            dve.wait_ge(pT_full, DC * B)
            free = prob[0:1].rearrange("p a c h m -> p (a c h m)")
            one, n_e, past, skip = (free[:, E * i:E * i + E] for i in range(4))
            passed, more = (free[:, first:first + a * b].rearrange("p (a b) -> p a b", a=a) for first, a, b in ((4 * E, TILES, E), (4 * E + TILES * E, E, B)))
            tab_f = free[:, 4 * E + (TILES + B) * E:4 * E + (TILES + B) * E + 3 * TILES].rearrange("p (r t) -> p r t", r=3)
            step = [0]

            def link(ins):
                step[0] += 1
                ins.then_inc(tab_step, 1)
                dve.wait_ge(tab_step, step[0])

            across = lambda t: t[:, :].unsqueeze(1).to_broadcast([1, TILES, E])
            link(nc.vector.memset(one[:, :], 1.0))
            link(tt(n_e[:, :], fill[0:1, 0, :], const[0:1, C_BASE:C_BASE + E], ALU.subtract))
            link(tt(more[:, :, :], n_e[:, :].unsqueeze(2).to_broadcast([1, E, B]),
                    const[0:1, C_MULT:C_MULT + B].unsqueeze(1).to_broadcast([1, E, B]), ALU.is_gt))
            link(nc.vector.tensor_reduce(n_e[:, :], more[:, :, :], axis=AX.X, op=ALU.add))
            link(nc.vector.tensor_tensor_scan(past[:, :], one[:, :], n_e[:, :], 0.0, ALU.mult, ALU.add))
            link(ts(skip[:, :], n_e[:, :], -float(P), float(LIST), ALU.mult, ALU.add))
            link(tt(passed[:, :, :], const[0:1, C_TILE:C_TILE + TILES].unsqueeze(2).to_broadcast([1, TILES, E]), across(past), ALU.is_ge))
            link(nc.vector.tensor_reduce(tab_f[:, 0, :], passed[:, :, :], axis=AX.X, op=ALU.add))
            link(tt(passed[:, :, :], passed[:, :, :], across(skip), ALU.mult))
            link(nc.vector.tensor_reduce(tab_f[:, 1, :], passed[:, :, :], axis=AX.X, op=ALU.add))
            tt(tab_f[:, 2, 0:1], tab_f[:, 0, 0:1], tab_f[:, 0, 0:1], ALU.is_equal)
            link(tt(tab_f[:, 2, 1:TILES], tab_f[:, 0, 1:TILES], tab_f[:, 0, 0:TILES - 1], ALU.not_equal))
            link(tt(tab_f[:, 2, :], tab_f[:, 2, :], const[0:1, C_DEP:C_DEP + TILES], ALU.add))
            ts(tab_f[:, 2, :], tab_f[:, 2, :], 16.0, None, ALU.mult)
            link(ts(tab_f[:, 0, :], tab_f[:, 0, :], float(E - 1), None, ALU.min))
            link(nc.vector.scalar_tensor_tensor(out=tab_f[:, 1, :], in0=const[0:1, C_TILE:C_TILE + TILES], scalar=float(P), in1=tab_f[:, 1, :],
                                                op0=ALU.mult, op1=ALU.add))
            link(nc.vector.tensor_copy(tab[:, :, :], tab_f[:, :, :]))

        @block.gpsimd
        def _(pool):
            tt, ts = nc.gpsimd.tensor_tensor, nc.gpsimd.tensor_scalar
            pool.memset(half[:, :], -0.5).then_inc(half_done, 1)
            for r in range(2):
                pool.memset(kblk[:, r].bitcast(f32), 0.0).then_inc(blocks_zeroed, 1)
            pool.wait_ge(half_done, 1)

            def hold(semaphore, value):
                pool.wait_ge(semaphore, value)
                pool.sem_inc(pool_held, 1)

            def rstd(step_sem, base, var, nwt, out_, var_in, n):
                ops = [lambda: ts(var, var_in, LN_EPS, None, ALU.add),
                       lambda: tt(out_, var, half[:, 0:n], ALU.pow),
                       lambda: tt(nwt, var, out_, ALU.mult),
                       lambda: tt(nwt, nwt, out_, ALU.mult),
                       lambda: ts(nwt, nwt, -0.5, 1.5, ALU.mult, ALU.add),
                       lambda: tt(out_, out_, nwt, ALU.mult)]
                for i, op in enumerate(ops):
                    op().then_inc(step_sem, 1)
                    if i < len(ops) - 1:
                        hold(step_sem, base(i + 1))

            def body(g):
                for j in range(4):
                    for c in range(DC):
                        b = graph(g, j - 1)
                        if b.valid and c < 2:
                            r = b.ring(2)
                            hold(rinv_step, b.count(4, 2 * c + 2))
                            for q in (2 * c, 2 * c + 1):
                                tt(prob[:, r, q], prob[:, r, q], rinv[:, r, HC * q:HC * q + HC].unsqueeze(2).to_broadcast([P, HC, P]), ALU.mult)\
                                    .then_inc(prob_done, 1)
                        if c == 0:
                            b = graph(g, j + 1)
                            if b.valid:
                                k = b.ring(4)
                                hold(bias_in[k], 16 * b.turn(4) + 16)
                                tt(bias[:, k, :], bias[:, k, :], bias[:, k, :], ALU.add).then_inc(bias_done, 1)
                        if c == 3 and j % 2:
                            p = pair(g, j - 4)
                            if p.valid:
                                hold(e_hi_done, p.count(1, 1))
                                tt(e_lo[:, :], e_stage[:, :], e_hi[:, :].bitcast(f32), ALU.subtract).then_inc(e_lo_done, 1)
                        if c == 3 and j % 2 == 0:
                            p = pair(g, j + 4)
                            if p.valid:
                                k = 2 * p.ring(2)
                                hold(mean1, p.count(2, 2))
                                if p.after(2):
                                    hold(xn_done, p.count(2, -2))
                                rstd(rstd1_step, lambda i, p=p: p.count(RSTD, i), var1[:, k:k + 2], nwt1[:, k:k + 2], rstd1[:, k:k + 2], mv1[:, k:k + 2, 1], 2)
                        if c == 2:
                            b = graph(g, j - 2)
                            if b.valid:
                                k = b.ring(4)
                                hold(mean2, b.count(1, 1))
                                rstd(rstd2_step, lambda i, b=b: b.count(RSTD, i), var2[:, k:k + 1], nwt2[:, k:k + 1], rstd2[:, k:k + 1], mv2[:, k, 1:2], 1)
                        a = j % 2
                        p = pair(g, j - 6 - a)
                        if c == 2 - a and p.valid:
                            if a == 0:
                                hold(place_step, p.count(PLACE, PLACE))
                                hold(route_step, p.count(ROUTE, ROUTE))
                            r = p.ring(2)
                            for k in range(K):
                                pool.indirect_dma_start(out=x_lists, out_offset=bass.IndirectOffsetOnAxis(ap=pos[:, r, k, a:a + 1], axis=0),
                                                        in_=xn2[:, 2 * r + a, :], in_offset=None).then_inc(scattered[a], 16)

            turns(pool, body)
            for a in range(2):
                pool.wait_ge(scattered[a], 32 * (B // 2))


def phase_b(nc, v):
    f32, f32r, i32 = v["f32"], v["f32r"], v["i32"]
    ALU, ACT, AX = v["ALU"], v["ACT"], v["AX"]
    sem, sems = v["sem"], v["sems"]
    const, ident, fill, ends, zero_tile, tab = v["const"], v["ident"], v["fill"], v["ends"], v["zero_tile"], v["tab"]
    x_lists, e_parts, out = v["x_lists"], v["e_parts"], v["out"]
    R = RING
    N = 2 * R

    mem = ExitStack()
    with mem:
        def sb(name, shape, dt=f32):
            return v["sb"](mem, name, shape, dt)

        we_hi = sb("we_hi", [P, E * DC * D], f32r)
        we_lo = sb("we_lo", [P, E * DC * D], f32r)
        e_bias = sb("e_bias", [P, E * D])
        xg = sb("xg", [P, N, W])
        xgT_hi = sb("xgT_hi", [P, R, DC, P], f32r)
        xgT_lo = sb("xgT_lo", [P, R, DC, P], f32r)
        token = sb("token", [P, N, 1], i32)
        comb = sb("comb", [P, N * E])
        yt = sb("yt", [P, R, D])
        ps_x = [v["pb"](mem, f"ps_x{i}", [P, 512], f32) for i in range(R)]
        ps_y = [v["pb"](mem, f"ps_y{i}", [P, 512], f32) for i in range(R)]

        ebias_in, parts_in = sem("ebias_in"), sems("parts_in", E)
        experts_in = sem("experts_in")
        xg_in, added = sems("xg_in", N), sems("added", R)
        xgT_full, xgT_hi_done, xgT_lo_done = sem("xgT_full"), sem("xgT_hi_done"), sem("xgT_lo_done")
        y_full, y_step = sem("y_full"), sem("y_step")
        meta_done, poolb_held = sem("meta_done"), sem("poolb_held")

        def tile(g, off):
            return Item(g, N, off, TILES)

        def turns(eng, body):
            body(-1)
            body(0)
            with eng.Fori(1, TILES // N - 1) as g:
                body(g)
            for g in range(TILES // N - 1, TILES // N + 2):
                body(g)

        block = mem.enter_context(nc.Block())

        @block.sync
        def _(sp):
            for e in range(E):
                for i, w in enumerate((we_hi, we_lo)):
                    sp.dma_start(w[:, e * DC * D:(e + 1) * DC * D].bitcast(f32).rearrange("p (c f) -> p c f", c=DC),
                                 e_parts[i, DC * e:DC * e + DC].rearrange("c p f -> p c f")).then_inc(parts_in[e], 16)
                    if e or i:
                        sp.wait_ge(parts_in[e], 16 * i + 16)
                sp.sem_inc(experts_in, 1)
                if e == 0:
                    sp.dma_start(e_bias[:, :], v["expert_b"].rearrange("(a e) f -> a (e f)", a=1).to_broadcast([P, E * D])).then_inc(ebias_in, 16)

        @block.tensor
        def _(pe):
            def body(g):
                for j in range(N):
                    t = tile(g, j + 1)
                    if t.valid:
                        r = t.ring(R)
                        pe.wait_ge(xg_in[t.ring(N)], 16 * t.turn(N) + 16)
                        if t.after(R):
                            pe.wait_ge(xgT_lo_done, t.count(1, 1 - R))
                        for c in range(DC):
                            last = nc.tensor.transpose(ps_x[r][:, P * c:P * c + P], xg[:, t.ring(N), P * c:P * c + P], ident)
                        last.then_inc(xgT_full, 1)
                    t = tile(g, j)
                    if t.valid:
                        r = t.ring(R)
                        e = pe.value_load(tab[0:1, 0, bass.ds(t.count(), 1)], min_val=0, max_val=E - 1)
                        pe.wait_ge(experts_in, e + 1)
                        pe.wait_ge(xgT_lo_done, t.count(1, 1))
                        if t.after(R):
                            pe.wait_ge(y_step, t.count(2, 1 - 2 * R))
                        for c in range(DC):
                            hi, lo = we_hi[:, bass.ds(e * (DC * D) + c * D, D)], we_lo[:, bass.ds(e * (DC * D) + c * D, D)]
                            nc.tensor.matmul(ps_y[r][:, :], xgT_hi[:, r, c, :], hi, start=c == 0, stop=False)
                            nc.tensor.matmul(ps_y[r][:, :], xgT_hi[:, r, c, :], lo, start=False, stop=False)
                            last = nc.tensor.matmul(ps_y[r][:, :], xgT_lo[:, r, c, :], hi, start=False, stop=c == DC - 1)
                        last.then_inc(y_full, 1)
            turns(pe, body)

        @block.scalar
        def _(act):
            def body(g):
                for j in range(N):
                    t = tile(g, j + 1)
                    if t.valid:
                        r = t.ring(R)
                        act.wait_ge(xgT_full, t.count(1, 1))
                        if t.after(R):
                            act.wait_ge(y_full, t.count(1, 1 - R))
                        nc.scalar.activation(xgT_hi[:, r].rearrange("p c t -> p (c t)"), ps_x[r][:, :], ACT.Copy).then_inc(xgT_hi_done, 1)
                    t = tile(g, j + N)
                    if t.valid:
                        row = act.value_load(tab[0:1, 1, bass.ds(t.count(), 1)], min_val=0, max_val=ROWS - P)
                        if t.after(N):
                            act.wait_ge(xgT_full, t.count(1, 1 - N))
                            act.wait_ge(meta_done, t.count(2, 2 - 2 * N))
                        act.dma_start(xg[:, t.ring(N), :], x_lists[bass.ds(row, P), :]).then_inc(xg_in[t.ring(N)], 16)
            turns(act, body)

        @block.vector
        def _(dve):
            tt, ts = nc.vector.tensor_tensor, nc.vector.tensor_scalar
            def body(g):
                for j in range(N):
                    t = tile(g, j + 1)
                    if t.valid:
                        r = t.ring(R)
                        dve.wait_ge(xgT_hi_done, t.count(1, 1))
                        tt(xgT_lo[:, r].rearrange("p c t -> p (c t)"), ps_x[r][:, :], xgT_hi[:, r].rearrange("p c t -> p (c t)").bitcast(f32),
                           ALU.subtract).then_inc(xgT_lo_done, 1)
                    t = tile(g, j - 1)
                    if t.valid:
                        r, m = t.ring(R), t.ring(N)
                        e = dve.value_load(tab[0:1, 0, bass.ds(t.count(), 1)], min_val=0, max_val=E - 1)
                        dve.wait_ge(y_full, t.count(1, 1))
                        if t.after(R):
                            dve.wait_ge(added[r], 16 * t.turn(R))
                        elif t.count() == 0:
                            dve.wait_ge(ebias_in, 16)
                        tt(yt[:, r, :], ps_y[r][:, :], e_bias[:, bass.ds(e * D, D)], ALU.add).then_inc(y_step, 1)
                        dve.wait_ge(meta_done, t.count(2, 2))
                        dve.wait_ge(y_step, t.count(2, 1))
                        ts(yt[:, r, :], yt[:, r, :], comb[:, bass.ds(e + E * m, 1)], None, ALU.mult).then_inc(y_step, 1)
            turns(dve, body)

        @block.gpsimd
        def _(pool):
            def hold(semaphore, value):
                pool.wait_ge(semaphore, value)
                pool.sem_inc(poolb_held, 1)

            def body(g):
                for j in range(N):
                    t = tile(g, j + 1)
                    if t.valid:
                        r, m = t.ring(R), t.ring(N)
                        hold(xg_in[m], 16 * t.turn(N) + 16)
                        if t.after(N):
                            hold(added[r], 16 * t.turn(R) - 16)
                        nc.gpsimd.tensor_copy(token[:, m, :], xg[:, m, D:D + 1]).then_inc(meta_done, 1)
                        nc.gpsimd.tensor_copy(comb[:, E * m:E * m + E], xg[:, m, D + 1:W]).then_inc(meta_done, 1)
                    t = tile(g, j - 1)
                    if t.valid:
                        r, m = t.ring(R), t.ring(N)
                        if t.after(2 * R):
                            need = pool.value_load(tab[0:1, 2, bass.ds(t.count(), 1)], min_val=16, max_val=16 * (TILES // R + 1))
                            hold(added[(j - 3) % R], 16 * tile(g, j - 3).turn(R) + 16)
                            hold(added[(j - 2) % R], need)
                        elif t.after(1):
                            pool.wait_ge(added[(j - 2) % R], 16 * tile(g, j - 2).turn(R) + 16)
                        hold(y_step, t.count(2, 2))
                        pool.indirect_dma_start(out=out, out_offset=bass.IndirectOffsetOnAxis(ap=token[:, m, :], axis=0),
                                                in_=yt[:, r, :], in_offset=None, compute_op=ALU.add).then_inc(added[r], 16)
            turns(pool, body)
            for r in range(R):
                pool.wait_ge(added[r], 16 * (TILES // R))


def constants():
    c = np.zeros((P, C_ALL), np.float32)
    c[:, C_ID:C_ID + P] = np.eye(P)
    for e in range(E):
        c[e::HD, C_SEL + e] = 1.0
    c[:, C_REV:C_REV + 2 * E] = np.tile(E - np.arange(E), 2)
    c[:, C_BASE:C_BASE + E] = LIST * np.arange(E)
    c[:, C_TRI:C_TRI + P] = np.arange(P)[:, None] < np.arange(P)[None, :]
    c[:, C_MULT:C_MULT + B] = P * np.arange(B)
    c[:, C_TILE:C_TILE + TILES] = np.arange(TILES)
    c[:, C_DEP:C_DEP + TILES] = (np.arange(TILES) - 1) // RING
    c[:, C_TOK:C_TOK + B] = P * np.arange(B) + np.arange(P)[:, None]
    c[:, C_DUM:C_DUM + E] = T + P * np.arange(E) + np.arange(P)[:, None]
    return c


def kernel(**inputs):
    import concourse.bacc as bacc
    from concourse.bass_utils import run_bass_kernel_spmd

    a = {n: np.asarray(t) for n, t in inputs.items()}
    arrays = {
        "x": a["x"], "adj": a["adj"],
        "WqT": a["L0_gnn_Wq"].T, "WkT": a["L0_gnn_Wk"].T, "WvT": a["L0_gnn_Wv"].T, "WoT": a["L0_gnn_Wo"].T,
        "gate_W": a["L0_ffn_gate_W"], "gate_b": a["L0_ffn_gate_b"],
        "expert_W": a["L0_ffn_expert_W"], "expert_b": a["L0_ffn_expert_b"],
        "consts": constants(),
    }
    arrays = {n: np.ascontiguousarray(t) for n, t in arrays.items()}
    nc = bacc.Bacc("TRN2", target_bir_lowering=False, num_devices=1)
    aps = {n: nc.dram_tensor(n, t.shape, mybir.dt.from_np(t.dtype), kind="ExternalInput").ap() for n, t in arrays.items()}
    out = nc.dram_tensor("out", (T + DUMMY, D), mybir.dt.float32, kind="ExternalOutput").ap()
    build(nc, *aps.values(), out)
    r = run_bass_kernel_spmd(nc, [arrays], core_ids=[0])
    return r.results[0]["out"][:T].reshape(B, P, D)
```
